# Optimizing a Trainium2 kernel written in Bass

```python
import numpy as np
import jax
import jax.numpy as jnp

def _softmax(x, axis=-1):
    return jax.nn.softmax(x, axis=axis)

def _gelu(x):
    return jax.nn.gelu(x, approximate=True)

def _silu(x):
    return jax.nn.silu(x)

def _sigmoid(x):
    return jax.nn.sigmoid(x)

def _layernorm(x, axis=-1, eps=1e-05):
    m = jnp.mean(x, axis=axis, keepdims=True)
    v = jnp.var(x, axis=axis, keepdims=True)
    return (x - m) / jnp.sqrt(v + eps)

def _scatter_add(tgt, idx, src, axis=0):
    return tgt.at[idx].add(src)

def _segment_sum(src, seg, n):
    return jax.ops.segment_sum(src, seg, n)
kernel_name = 'mk_gnn_preln_d4_gnn_r8_02edcb'

def setup_inputs(seed: int=0):
    np.random.seed(seed)
    _w = jnp.asarray

    def _rec_inputs():
        import jax
        import jax.numpy as jnp
        _gk = jax.random.key(seed)
        x = -0.000202 + 1 * jax.random.normal(jax.random.fold_in(_gk, 1), (6250, 128), jnp.float32)
        _s = jax.random.randint(jax.random.fold_in(_gk, 2), (100000,), 0, 6250, jnp.int32)
        _d = jax.random.randint(jax.random.fold_in(_gk, 3), (100000,), 0, 6250, jnp.int32)
        _loop = jnp.arange(6250, dtype=jnp.int32)
        src = jnp.concatenate([_s, _d, _loop])
        dst = jnp.concatenate([_d, _s, _loop])
        _o = jnp.argsort(dst, stable=True)
        src = src[_o]
        dst = dst[_o]
        edge_attr_2 = jax.random.uniform(jax.random.fold_in(_gk, 12), (206250, 2), jnp.float32, 0.0, 0.999999)
        edge_attr_5 = 0.000254407 + 0.99978 * jax.random.normal(jax.random.fold_in(_gk, 13), (206250, 5), jnp.float32)
        edge_weight = 0.00107675 + 0.999702 * jax.random.normal(jax.random.fold_in(_gk, 15), (206250,), jnp.float32)
        return (x, src, dst, edge_attr_2, edge_attr_5, edge_weight)
    x, src, dst, edge_attr_2, edge_attr_5, edge_weight = _rec_inputs()

    def _L0_gnn_setup():
        import jax, jax.numpy as jnp
        import numpy as np
        import math
        N_NODES, N_EDGES, DIM, N_HEADS = (6250, 100000, 128, 8)
        D_K = DIM // N_HEADS
        key = jax.random.key(seed)
        ks = jax.random.split(key, 12)
        f32 = jnp.float32
        s = 1.0 / math.sqrt(DIM)
        return {'x': jax.random.normal(ks[0], (N_NODES, DIM), f32), 'src': jax.random.randint(ks[1], (N_EDGES,), 0, N_NODES), 'dst': jax.random.randint(ks[2], (N_EDGES,), 0, N_NODES), 'edge_weight': jax.random.normal(ks[3], (N_EDGES,), f32), 'Wk': jax.random.normal(ks[4], (DIM, DIM), f32) * s, 'bk': jax.random.normal(ks[5], (DIM,), f32) * 0.01, 'Wq': jax.random.normal(ks[6], (DIM, DIM), f32) * s, 'bq': jax.random.normal(ks[7], (DIM,), f32) * 0.01, 'Wv': jax.random.normal(ks[8], (DIM, DIM), f32) * s, 'bv': jax.random.normal(ks[9], (DIM,), f32) * 0.01, 'rel_att': jax.random.normal(ks[10], (N_HEADS, D_K), f32) * 0.1, 'rel_msg': jax.random.normal(ks[11], (N_HEADS, D_K, D_K), f32) / math.sqrt(D_K)}
    _L0_gnn_all = _L0_gnn_setup()
    _L0_gnn_in = {k: v for k, v in _L0_gnn_all.items() if k in ('Wk', 'bk', 'Wq', 'bq', 'Wv', 'bv', 'rel_att', 'rel_msg')}
    del _L0_gnn_all

    def _L1_gnn_setup():
        import jax, jax.numpy as jnp
        import numpy as np
        N_NODES = 12500
        N_EDGES = 200000
        D_IN = 128
        D_MSG = 128
        D_HID = 128
        D_EDGE = 5
        D_CAT = D_IN + D_MSG
        D_U1, D_U2, D_OUT = (214, 172, 128)

        def _leaky(x):
            return jax.nn.leaky_relu(x, negative_slope=0.01)
        key = jax.random.key(seed)
        ks = jax.random.split(key, 12)

        def kaiming(k, shape):
            fan_in = shape[1]
            gain = np.sqrt(2.0 / (1.0 + 0.01 ** 2))
            return jax.random.normal(k, shape, dtype=jnp.float32) * (gain / np.sqrt(fan_in))
        x = jax.random.normal(ks[0], (N_NODES, D_IN), dtype=jnp.float32)
        edge_index = jax.random.randint(ks[1], (2, N_EDGES), 0, N_NODES, dtype=jnp.int64)
        edge_attr = jax.random.normal(ks[2], (N_EDGES, D_EDGE), dtype=jnp.float32)
        return {'x': x, 'edge_index': edge_index, 'edge_attr': edge_attr, 'Wm1': kaiming(ks[3], (D_HID, D_EDGE)), 'bm1': jnp.zeros((D_HID,), jnp.float32), 'Wm2': kaiming(ks[4], (D_HID, D_HID)), 'bm2': jnp.zeros((D_HID,), jnp.float32), 'Wm3': kaiming(ks[5], (D_MSG, D_HID)), 'bm3': jnp.zeros((D_MSG,), jnp.float32), 'ln_g': jnp.ones((D_CAT,), jnp.float32), 'ln_b': jnp.zeros((D_CAT,), jnp.float32), 'Wu1': kaiming(ks[6], (D_U1, D_CAT)), 'bu1': jnp.zeros((D_U1,), jnp.float32), 'Wu2': kaiming(ks[7], (D_U2, D_U1)), 'bu2': jnp.zeros((D_U2,), jnp.float32), 'Wu3': kaiming(ks[8], (D_OUT, D_U2)), 'bu3': jnp.zeros((D_OUT,), jnp.float32)}
    _L1_gnn_all = _L1_gnn_setup()
    _L1_gnn_in = {k: v for k, v in _L1_gnn_all.items() if k in ('Wm1', 'bm1', 'Wm2', 'bm2', 'Wm3', 'bm3', 'ln_g', 'ln_b', 'Wu1', 'bu1', 'Wu2', 'bu2', 'Wu3', 'bu3')}
    del _L1_gnn_all

    def _L2_gnn_setup():
        import jax, jax.numpy as jnp
        import numpy as np
        NEG_SLOPE = 0.2
        key = jax.random.key(seed)
        ks = jax.random.split(key, 8)
        N, IN, H, C = (6250, 128, 4, 32)
        E = 100000
        TD = H * C
        x = jax.random.normal(ks[0], (N, IN), dtype=jnp.float32)
        edge_index = jax.random.randint(ks[1], (2, E), 0, N, dtype=jnp.int64)
        edge_attr = jax.random.uniform(ks[2], (E, 2), dtype=jnp.float32)
        W_lin = jax.random.normal(ks[3], (TD, IN), dtype=jnp.float32) * (2.0 / (IN + TD)) ** 0.5
        att = jax.random.normal(ks[4], (H, C), dtype=jnp.float32) * (2.0 / (H + C)) ** 0.5
        W_eb = jax.random.normal(ks[5], (H, 1), dtype=jnp.float32) * (2.0 / (H + 1)) ** 0.5
        bias = jnp.zeros((TD,), dtype=jnp.float32)
        W_res = jax.random.normal(ks[6], (TD, IN), dtype=jnp.float32) * (2.0 / (IN + TD)) ** 0.5
        return {'x': x, 'edge_index': edge_index, 'edge_attr': edge_attr, 'W_lin': W_lin, 'att': att, 'W_eb': W_eb, 'bias': bias, 'W_res': W_res}
    _L2_gnn_all = _L2_gnn_setup()
    _L2_gnn_in = {k: v for k, v in _L2_gnn_all.items() if k in ('W_lin', 'att', 'W_eb', 'bias', 'W_res')}
    del _L2_gnn_all

    def _L3_gnn_setup():
        import jax, jax.numpy as jnp
        import numpy as np
        NEG_SLOPE = 0.2
        key = jax.random.key(seed)
        k1, k2, k3, k4, k5 = jax.random.split(key, 5)
        N, E = (6250, 100000)
        IN, H, O = (128, 4, 32)
        x = jax.random.normal(k1, (N, IN), dtype=jnp.float32)
        edge_index = jax.random.randint(k2, (2, E), 0, N, dtype=jnp.int64)
        weight = jax.random.normal(k3, (IN, H, O), dtype=jnp.float32) * 0.05
        att_weight = jax.random.normal(k4, (H, 2 * O), dtype=jnp.float32) * 0.05
        bias = jax.random.normal(k5, (H * O,), dtype=jnp.float32) * 0.05
        return {'x': x, 'edge_index': edge_index, 'weight': weight, 'att_weight': att_weight, 'bias': bias}
    _L3_gnn_all = _L3_gnn_setup()
    _L3_gnn_in = {k: v for k, v in _L3_gnn_all.items() if k in ('weight', 'att_weight', 'bias')}
    del _L3_gnn_all
    return {'x': x, 'src': src, 'dst': dst, 'edge_attr_2': edge_attr_2, 'edge_attr_5': edge_attr_5, 'edge_weight': edge_weight, 'L0_gnn_Wk': _L0_gnn_in['Wk'], 'L0_gnn_bk': _L0_gnn_in['bk'], 'L0_gnn_Wq': _L0_gnn_in['Wq'], 'L0_gnn_bq': _L0_gnn_in['bq'], 'L0_gnn_Wv': _L0_gnn_in['Wv'], 'L0_gnn_bv': _L0_gnn_in['bv'], 'L0_gnn_rel_att': _L0_gnn_in['rel_att'], 'L0_gnn_rel_msg': _L0_gnn_in['rel_msg'], 'L1_gnn_Wm1': _L1_gnn_in['Wm1'], 'L1_gnn_bm1': _L1_gnn_in['bm1'], 'L1_gnn_Wm2': _L1_gnn_in['Wm2'], 'L1_gnn_bm2': _L1_gnn_in['bm2'], 'L1_gnn_Wm3': _L1_gnn_in['Wm3'], 'L1_gnn_bm3': _L1_gnn_in['bm3'], 'L1_gnn_ln_g': _L1_gnn_in['ln_g'], 'L1_gnn_ln_b': _L1_gnn_in['ln_b'], 'L1_gnn_Wu1': _L1_gnn_in['Wu1'], 'L1_gnn_bu1': _L1_gnn_in['bu1'], 'L1_gnn_Wu2': _L1_gnn_in['Wu2'], 'L1_gnn_bu2': _L1_gnn_in['bu2'], 'L1_gnn_Wu3': _L1_gnn_in['Wu3'], 'L1_gnn_bu3': _L1_gnn_in['bu3'], 'L2_gnn_W_lin': _L2_gnn_in['W_lin'], 'L2_gnn_att': _L2_gnn_in['att'], 'L2_gnn_W_eb': _L2_gnn_in['W_eb'], 'L2_gnn_bias': _L2_gnn_in['bias'], 'L2_gnn_W_res': _L2_gnn_in['W_res'], 'L3_gnn_weight': _L3_gnn_in['weight'], 'L3_gnn_att_weight': _L3_gnn_in['att_weight'], 'L3_gnn_bias': _L3_gnn_in['bias']}

def reference(x, src, dst, edge_attr_2, edge_attr_5, edge_weight, L0_gnn_Wk, L0_gnn_bk, L0_gnn_Wq, L0_gnn_bq, L0_gnn_Wv, L0_gnn_bv, L0_gnn_rel_att, L0_gnn_rel_msg, L1_gnn_Wm1, L1_gnn_bm1, L1_gnn_Wm2, L1_gnn_bm2, L1_gnn_Wm3, L1_gnn_bm3, L1_gnn_ln_g, L1_gnn_ln_b, L1_gnn_Wu1, L1_gnn_bu1, L1_gnn_Wu2, L1_gnn_bu2, L1_gnn_Wu3, L1_gnn_bu3, L2_gnn_W_lin, L2_gnn_att, L2_gnn_W_eb, L2_gnn_bias, L2_gnn_W_res, L3_gnn_weight, L3_gnn_att_weight, L3_gnn_bias):
    import jax
    import jax.numpy as jnp

    def _L0_gnn_ref(x, src, dst, edge_weight, Wk, bk, Wq, bq, Wv, bv, rel_att, rel_msg):
        import jax, jax.numpy as jnp
        import numpy as np
        import math
        N_NODES, N_EDGES, DIM, N_HEADS = (6250, 100000, 128, 8)
        D_K = DIM // N_HEADS
        N, D = x.shape
        H, dk = rel_att.shape
        inv_sqrt_dk = jnp.asarray(1.0 / math.sqrt(dk), x.dtype)
        k = (x @ Wk.T + bk).reshape(N, H, dk)
        q = (x @ Wq.T + bq).reshape(N, H, dk)
        v = (x @ Wv.T + bv).reshape(N, H, dk)
        qp = edge_weight[:, None, None] * rel_att[None]
        att = ((q[dst] + qp) * k[src]).sum(-1) * inv_sqrt_dk
        val = jnp.einsum('ehd,hdk->ehk', v[src], rel_msg)
        m = jax.ops.segment_max(att, dst, num_segments=N)
        e = jnp.exp(att - m[dst])
        s = jax.ops.segment_sum(e, dst, num_segments=N)
        w = e / s[dst]
        h = jax.ops.segment_sum(w[..., None] * val, dst, num_segments=N)
        return jax.nn.relu(h.reshape(N, D))

    def _L1_gnn_ref(x, edge_index, edge_attr, Wm1, bm1, Wm2, bm2, Wm3, bm3, ln_g, ln_b, Wu1, bu1, Wu2, bu2, Wu3, bu3):
        import jax, jax.numpy as jnp
        import numpy as np
        N_NODES = 12500
        N_EDGES = 200000
        D_IN = 128
        D_MSG = 128
        D_HID = 128
        D_EDGE = 5
        D_CAT = D_IN + D_MSG
        D_U1, D_U2, D_OUT = (214, 172, 128)

        def _leaky(x):
            return jax.nn.leaky_relu(x, negative_slope=0.01)
        h = _leaky(edge_attr @ Wm1.T + bm1)
        h = _leaky(h @ Wm2.T + bm2)
        msg = h @ Wm3.T + bm3
        dst = edge_index[1]
        aggr = jax.ops.segment_sum(msg, dst, num_segments=x.shape[0])
        cat = jnp.concatenate([x, aggr], axis=-1)
        mu = jnp.mean(cat, axis=-1, keepdims=True)
        var = jnp.mean((cat - mu) ** 2, axis=-1, keepdims=True)
        nrm = (cat - mu) * jax.lax.rsqrt(var + 1e-05) * ln_g + ln_b
        u = _leaky(nrm @ Wu1.T + bu1)
        u = _leaky(u @ Wu2.T + bu2)
        return u @ Wu3.T + bu3

    def _L2_gnn_ref(x, edge_index, edge_attr, W_lin, att, W_eb, bias, W_res):
        import jax, jax.numpy as jnp
        import numpy as np
        NEG_SLOPE = 0.2
        N = x.shape[0]
        H, C = att.shape
        reduced = edge_attr[:, 0] + 0.35 * edge_attr[:, 1]
        loops = jnp.arange(N, dtype=edge_index.dtype)
        src = jnp.concatenate([edge_index[0], loops])
        dst = jnp.concatenate([edge_index[1], loops])
        reduced = jnp.concatenate([reduced, jnp.ones((N,), dtype=x.dtype)])
        proj = (x @ W_lin.T).reshape(N, H, C)
        ps = proj[src]
        pd = proj[dst]
        z = jax.nn.leaky_relu(ps + pd, negative_slope=NEG_SLOPE)
        logits = jnp.einsum('ehc,hc->eh', z, att) + reduced[:, None] * W_eb[:, 0][None, :]
        mx = jax.ops.segment_max(logits, dst, num_segments=N)
        e = jnp.exp(logits - mx[dst])
        denom = jax.ops.segment_sum(e, dst, num_segments=N)
        attn = e / jnp.maximum(denom[dst], 1e-12)
        msg = attn[:, :, None] * ps
        out = jax.ops.segment_sum(msg, dst, num_segments=N)
        out = out.reshape(N, H * C)
        out = out + x @ W_res.T
        return out + bias

    def _L3_gnn_ref(x, edge_index, weight, att_weight, bias):
        import jax, jax.numpy as jnp
        import numpy as np
        NEG_SLOPE = 0.2
        N = x.shape[0]
        H, O = (weight.shape[1], weight.shape[2])
        h = jnp.einsum('ni,iho->nho', x, weight)
        src, dst = (edge_index[0], edge_index[1])
        h_i = h[dst]
        h_j = h[src]
        a_i, a_j = (att_weight[:, :O], att_weight[:, O:])
        alpha = jnp.einsum('eho,ho->eh', h_i, a_i) + jnp.einsum('eho,ho->eh', h_j, a_j)
        alpha = jax.nn.leaky_relu(alpha, NEG_SLOPE)
        amax = jax.ops.segment_max(alpha, dst, num_segments=N)
        ex = jnp.exp(alpha - amax[dst])
        denom = jax.ops.segment_sum(ex, dst, num_segments=N)
        coef = ex / (denom[dst] + 1e-16)
        out = jax.ops.segment_sum(h_j * coef[..., None], dst, num_segments=N)
        out = out.reshape(N, H * O) + bias
        return out
    edge_index = jnp.stack([src, dst])
    h = jnp.maximum(_layernorm(x, axis=-1), 0.0)
    x = x + _L0_gnn_ref(h, src, dst, edge_weight, L0_gnn_Wk, L0_gnn_bk, L0_gnn_Wq, L0_gnn_bq, L0_gnn_Wv, L0_gnn_bv, L0_gnn_rel_att, L0_gnn_rel_msg)
    h = jnp.maximum(_layernorm(x, axis=-1), 0.0)
    x = x + _L1_gnn_ref(h, edge_index, edge_attr_5, L1_gnn_Wm1, L1_gnn_bm1, L1_gnn_Wm2, L1_gnn_bm2, L1_gnn_Wm3, L1_gnn_bm3, L1_gnn_ln_g, L1_gnn_ln_b, L1_gnn_Wu1, L1_gnn_bu1, L1_gnn_Wu2, L1_gnn_bu2, L1_gnn_Wu3, L1_gnn_bu3)
    h = jnp.maximum(_layernorm(x, axis=-1), 0.0)
    x = x + _L2_gnn_ref(h, edge_index, edge_attr_2, L2_gnn_W_lin, L2_gnn_att, L2_gnn_W_eb, L2_gnn_bias, L2_gnn_W_res)
    h = jnp.maximum(_layernorm(x, axis=-1), 0.0)
    x = x + _L3_gnn_ref(h, edge_index, L3_gnn_weight, L3_gnn_att_weight, L3_gnn_bias)
    return x

_drawn_inputs = setup_inputs


def setup_inputs(seed=0):
    import zlib

    import numpy as np

    out = dict(_drawn_inputs(seed))
    spreads = {'L1_gnn_bm1': (0.0, 0.1),
     'L1_gnn_bm2': (0.0, 0.1),
     'L1_gnn_bm3': (0.0, 0.1),
     'L1_gnn_ln_g': (1.0, 0.2),
     'L1_gnn_ln_b': (0.0, 0.1),
     'L1_gnn_bu1': (0.0, 0.1),
     'L1_gnn_bu2': (0.0, 0.1),
     'L1_gnn_bu3': (0.0, 0.1),
     'L2_gnn_bias': (0.0, 0.1)}
    factors = {'edge_attr_2': 8.0,
     'edge_weight': 8.0,
     'L0_gnn_Wk': 2.903,
     'L0_gnn_bk': 8.0,
     'L0_gnn_Wq': 3.037,
     'L0_gnn_bq': 64.0,
     'L0_gnn_bv': 8.0,
     'L0_gnn_rel_att': 8.0,
     'L2_gnn_att': 3.654,
     'L2_gnn_W_eb': 8.0,
     'L3_gnn_att_weight': 55.556}
    for name, (base, spread) in spreads.items():
        noise = np.random.default_rng([zlib.crc32(name.encode()), seed]).standard_normal(out[name].shape)
        drawn = base * np.exp(spread * noise) if base else spread * noise
        out[name] = jnp.asarray(drawn.astype(out[name].dtype))
    for name, factor in factors.items():
        out[name] = (out[name] * factor).astype(out[name].dtype)
    return out
```

```python
from contextlib import ExitStack

import concourse.bass as bass
from concourse import mybir

ALU = mybir.AluOpType
ACT = mybir.ActivationFunctionType
F32 = mybir.dt.float32
I32 = mybir.dt.int32
BF16 = mybir.dt.bfloat16
AX = mybir.AxisListType

P = 128
N = 6250
E = 206250
D = 128
NB = -(-N // P) + 1
NBX = NB + 2
NP = NB * P
EC = -(-E // P)
EP = EC * P
RUNS = 4
RUN = EC // RUNS
assert RUN * RUNS == EC
ELAST = E - (P - 1) * EC
CH = 6
REC = 8
GROW = CH * REC
U = 4
SLAB = 512
SLABS = -(-(E // CH + 2 * NB + 4 * U) // SLAB)
NCMAX = SLABS * SLAB
LEAD = 3
MX = 6 * CH
H0, K0 = 8, 16
H2, K2 = 4, 32
V0 = H0 * (K0 + 1)
V2 = H2 * (K2 + 1)
ROW0 = D + H0 + V0
ROW2 = V2 + H2
BIG = 1.0e30
FLOOR = -1.0e29
RESET = -2.0e29
HUGE = 3.0e38
EPS = 1e-5
U1, U2 = 214, 172


class Tick:

    def __init__(self, sem, by=1):
        self.sem, self.by, self.n = sem, by, 0

    def __call__(self, ins):
        self.n += self.by
        ins.then_inc(self.sem, self.by)
        return self.n


def program(nc, dbg, x, src, dst, ea2, ea5, ew, w, out):
    ctx = ExitStack()
    with ctx:
        def sb(name, shape, dt=F32):
            return ctx.enter_context(nc.sbuf_tensor(name, shape, dt))

        def phase(stage, *args):
            with nc.cleanup_on_exit():
                stage(nc, t, s, *args)

        def dram(name, shape, dt=F32):
            return nc.dram_tensor(name, shape, dt, kind="Internal").ap()

        t = {}
        t["dstf"] = dram("dst_runs", [P * RUNS, RUN])
        t["recs"] = dram("edge_records", [EP, GROW])
        t["info"] = dram("node_rows", [NP, D + 4])
        t["tab"] = dram("chunk_tab", [P, NCMAX * 4], I32)
        t["blk"] = dram("chunk_blk", [1, NCMAX + LEAD], I32)
        t["meta"] = dram("chunk_meta", [NCMAX, P, 2 * CH], I32)
        t["row0"] = dram("rows0", [NP, ROW0])
        t["row2"] = dram("rows2", [NP, ROW2])
        t["row3"] = dram("rows3", [NP, ROW2])
        t["fin"] = dram("final", [NP, D])
        s = {}
        s["ident"] = sb("ident", [P, P])
        s["ones"] = sb("ones", [P, P])
        s["xp"] = sb("xp", [P, NBX, D])
        s["nid"] = sb("nid", [P, NB], I32)
        s["degp"] = sb("degp", [P, NB])
        s["ptrp"] = sb("ptrp", [P, NB])
        s["eps"] = sb("eps", [P, 1])
        s["cnt"] = sb("cnt", [1, 4], I32)
        phase(prep, dst, src, ew, ea2, ea5, x)
        phase(chunk_tables)
        s["tgt"] = sb("tgt", [P, NB, D])
        s["tsc"] = sb("tsc", [P, NB, H2])
        phase(project_rows, 0, w)
        s["acc"] = sb("acc", [P, NB, V0])
        s["msg"] = sb("msg", [P, NB, P])
        phase(edges_layer0, w)
        phase(node_mlp, w)
        phase(project_rows, 2, w)
        phase(edge_attention, 2, w, None)
        phase(project_rows, 3, w)
        phase(edge_attention, 3, w, out)
        if dbg is not None:
            dbg(nc, t, s)


def prep(nc, t, s, dst, src, ew, ea2, ea5, x):
    with ExitStack() as ctx:
        def sb(name, shape, dt=F32):
            return ctx.enter_context(nc.sbuf_tensor(name, shape, dt))

        def sem(name):
            return nc.alloc_semaphore(name)

        W = EC + CH - 1
        Q = 52
        NQ = EC // Q
        assert NQ * Q == EC
        dsti = sb("dsti", [P, EC], I32)
        dstr = sb("dstr", [P, EC])
        srci = sb("srci", [P, W], I32)
        wgt = sb("wgt", [P, W])
        at2 = sb("at2", [P, W, 2])
        at5 = sb("at5", [P, W, 5])
        rowq = sb("rowq", [P, 2, Q, GROW])
        fi = sb("iota_free", [P, P])
        pi = sb("iota_part", [P, 1])
        ltri = sb("ltri", [P, P], BF16)
        oneb = sb("oneb", [P, P], BF16)
        sh1 = sb("shift1", [P, P])
        sh2 = sb("shift2", [P, P])
        nval = sb("nval", [P, NB])
        lastr = sb("lastr", [P, RUNS * P])
        scr = sb("scr", [P, RUNS * P])
        cix = sb("cix", [P, NB])
        cii = sb("cii", [P, NB], I32)
        cnt = sb("fine", [P, NB])
        drow = sb("drow", [P, 10, RUN])
        ptr = sb("ptr", [P, NB + 1])
        deg = sb("deg", [P, NB])
        dv = sb("dv", [P, NB])
        oh = sb("oh", [P, NB, P], BF16)
        cum = sb("cum", [P, NB + 1, P], BF16)
        tot = sb("tot", [P, P])
        zero = sb("zero", [P, P])
        base = sb("base", [P, P])
        pre = sb("pre", [P, 2, 4 * P])
        scr2 = sb("scr2", [P, P])
        rank = sb("rank", [P, NB])
        ranki = sb("ranki", [P, NB], I32)
        info = sb("info", [P, NB, D + 4])
        infp = sb("infp", [P, NB, 4])
        ps = ctx.enter_context(nc.psum_tensor("ps_prep", [P, 4, 512], F32))

        ld_dst, ld_edge = sem("ld_dst"), sem("ld_edge")
        dst_out, pads = sem("dst_out"), sem("pads")
        iotas = sem("iotas")
        vec = Tick(sem("prep_vec"))
        mat = Tick(sem("prep_mat"))
        got_row = [sem(f"got_row{b}") for b in range(10)]
        rows_out = [sem(f"rows_out{b}") for b in range(2)]
        piece = sem("piece")
        counted = sem("counted")
        sorted_out, info_in, x_in = sem("sorted_out"), sem("info_in"), sem("x_in")
        at = {}

        def overlapped(a, width):
            return bass.AP(tensor=a.tensor, offset=0, ap=[[EC * width, P - 1], [1, W * width]])

        block = ctx.enter_context(nc.Block())

        @block.vector
        def _(v):
            def do(ins, key=None):
                n = vec(ins)
                if key:
                    at[key] = n
                return n

            do(nc.vector.memset(dsti[:], 1 << 20), "pad_dst")
            do(nc.vector.memset(s["ones"][:], 1.0))
            do(nc.vector.memset(s["eps"][:], EPS))
            do(nc.vector.memset(s["xp"][:, NB:NBX, :], 0.0))
            do(nc.vector.memset(oneb[:], 1.0))
            do(nc.vector.memset(zero[:], 0.0))
            do(nc.vector.memset(ptr[:, NB:NB + 1], float(E)))
            do(nc.vector.memset(info[:, NB - 2:NB, :], 0.0), "pad_x")
            v.wait_ge(iotas, 3)
            do(nc.vector.tensor_scalar(s["ident"][:], fi[:], pi[:, 0:1], None, ALU.is_equal))
            do(nc.vector.tensor_scalar(ltri[:], fi[:], pi[:, 0:1], None, ALU.is_gt))
            do(nc.vector.tensor_scalar(sh1[:], fi[:], 1.0, pi[:, 0:1], ALU.add, ALU.is_equal))
            do(nc.vector.tensor_scalar(sh2[:], fi[:], 1.0 - P, pi[:, 0:1], ALU.add, ALU.is_equal), "mats")
            v.wait_ge(ld_dst, 32)
            do(nc.vector.tensor_copy(dstr[:], dsti[:]), "dstr")
            v.wait_ge(mat.sem, 1)
            v.wait_ge(vec.sem, vec.n)
            do(nc.vector.tensor_copy(lastr[:], ps[:, 0, :]), "lastr")
            v.wait_ge(vec.sem, vec.n)
            for b in range(NB):
                do(nc.vector.scalar_tensor_tensor(scr[:], lastr[:], nval[:, b:b + 1], s["ones"][:, 0:1].to_broadcast([P, RUNS * P]),
                                                  ALU.is_lt, ALU.mult, accum_out=cix[:, b:b + 1]))
                v.wait_ge(vec.sem, vec.n)
            do(nc.vector.tensor_scalar(cix[:], cix[:], RUNS * P - 1.0, None, ALU.min))
            v.wait_ge(vec.sem, vec.n)
            do(nc.vector.tensor_copy(cii[:], cix[:]), "cii")
            v.wait_ge(ld_edge, 16 * 8)
            do(nc.vector.scalar_tensor_tensor(at2[:, :, 0], at2[:, :, 1], 0.35, at2[:, :, 0], ALU.mult, ALU.add), "reduced")
            for b in range(NB):
                v.wait_ge(got_row[b % 10], 16 * (b // 10 + 1))
                v.wait_ge(vec.sem, vec.n)
                do(nc.vector.scalar_tensor_tensor(scr[:, 0:RUN], drow[:, b % 10, :], nval[:, b:b + 1],
                                                  s["ones"][:, 0:1].to_broadcast([P, RUN]), ALU.is_lt, ALU.mult,
                                                  accum_out=cnt[:, b:b + 1]), ("fine", b))
            v.wait_ge(vec.sem, vec.n)
            do(nc.vector.scalar_tensor_tensor(ptr[:, 0:NB], cix[:], float(RUN), cnt[:], ALU.mult, ALU.add), "ptr")
            v.wait_ge(mat.sem, 2)
            v.wait_ge(vec.sem, vec.n)
            do(nc.vector.tensor_tensor(deg[:], ps[:, 1, 0:NB], ptr[:, 0:NB], ALU.subtract))
            v.wait_ge(vec.sem, vec.n)
            do(nc.vector.tensor_scalar(dv[:], deg[:], P - 1.0, -1.0, ALU.min, ALU.mult))
            v.wait_ge(vec.sem, vec.n)
            do(nc.vector.tensor_scalar(dv[:], dv[:], P - 1.0, None, ALU.add))
            do(nc.vector.memset(cum[:, 0, :], 0.0))
            v.wait_ge(vec.sem, vec.n)
            for b in range(NB):
                do(nc.vector.tensor_scalar(oh[:, b, :], fi[:], dv[:, b:b + 1], None, ALU.is_equal))
                v.wait_ge(vec.sem, vec.n)
                do(nc.vector.tensor_tensor(cum[:, b + 1, :], cum[:, b, :], oh[:, b, :], ALU.add), ("cum", b))
            v.wait_ge(mat.sem, 3)
            do(nc.vector.tensor_copy(tot[:], ps[:, 0, 0:P]))
            v.wait_ge(vec.sem, vec.n)
            do(nc.vector.tensor_tensor_scan(base[:], tot[:], zero[:], 0.0, ALU.add, ALU.add))
            v.wait_ge(vec.sem, vec.n)
            do(nc.vector.tensor_tensor(base[:], base[:], tot[:], ALU.subtract))
            for g in range(-(-NB // 4)):
                k = min(4, NB - 4 * g)
                v.wait_ge(mat.sem, 4 + g)
                v.wait_ge(vec.sem, vec.n)
                pr = pre[:, g % 2, :].rearrange("p (a b) -> p a b", a=4)
                do(nc.vector.tensor_tensor(pr[:, 0:k, :], ps[:, 2 + g % 2, 0:k * P].rearrange("p (a b) -> p a b", a=k),
                                           base[:].unsqueeze(1).to_broadcast([P, k, P]), ALU.add), ("pre", g))
                v.wait_ge(vec.sem, vec.n)
                for j in range(k):
                    b = 4 * g + j
                    do(nc.vector.tensor_tensor_reduce(scr2[:], oh[:, b, :], pr[:, j, :], 1.0, 0.0, ALU.mult,
                                                      ALU.add, rank[:, b:b + 1]))
                    v.wait_ge(vec.sem, vec.n)
            do(nc.vector.tensor_copy(ranki[:], rank[:]))
            do(nc.vector.tensor_copy(info[:, :, D:D + 1], nval[:].unsqueeze(2)))
            do(nc.vector.tensor_copy(info[:, :, D + 1:D + 2], ptr[:, 0:NB].unsqueeze(2)))
            do(nc.vector.tensor_copy(info[:, :, D + 2:D + 3], deg[:].unsqueeze(2)))
            do(nc.vector.memset(info[:, :, D + 3:D + 4], 0.0), "info")
            v.wait_ge(info_in, 32)
            do(nc.vector.tensor_copy(s["nid"][:], infp[:, :, 0]))
            do(nc.vector.tensor_copy(s["degp"][:], infp[:, :, 2]))
            do(nc.vector.tensor_copy(s["ptrp"][:], infp[:, :, 1]))

        @block.gpsimd
        def _(p):
            nc.gpsimd.iota(fi[:], [[1, P]], base=0, channel_multiplier=0, allow_small_or_imprecise_dtypes=True).then_inc(iotas, 1)
            nc.gpsimd.iota(pi[:], [[1, 1]], base=0, channel_multiplier=1, allow_small_or_imprecise_dtypes=True).then_inc(iotas, 1)
            nc.gpsimd.iota(nval[:], [[P, NB]], base=0, channel_multiplier=1, allow_small_or_imprecise_dtypes=True).then_inc(iotas, 1)
            for tile in (srci, wgt, at2, at5):
                nc.gpsimd.memset(tile[:], 0.0).then_inc(pads, 1)
            p.wait_ge(dst_out, 16)
            p.wait_ge(vec.sem, at["cii"])
            for b in range(NB):
                if b >= 10:
                    p.wait_ge(vec.sem, at["fine", b - 10])
                nc.gpsimd.indirect_dma_start(out=drow[:, b % 10, :], out_offset=None, in_=t["dstf"],
                                             in_offset=bass.IndirectOffsetOnAxis(ap=cii[:, b:b + 1], axis=0),
                                             ).then_inc(got_row[b % 10], 16)
            p.wait_ge(vec.sem, at["info"])
            p.wait_ge(x_in, 32)
            for b in range(NB):
                nc.gpsimd.indirect_dma_start(out=t["info"], out_offset=bass.IndirectOffsetOnAxis(ap=ranki[:, b:b + 1], axis=0),
                                             in_=info[:, b, :], in_offset=None).then_inc(sorted_out, 16)

        @block.tensor
        def _(pe):
            pe.wait_ge(vec.sem, at["dstr"])
            for r in range(RUNS):
                e = (r + 1) * RUN - 1
                mm = nc.tensor.matmul(ps[:, 0, r * P:(r + 1) * P], dstr[:, e:e + 1].to_broadcast([P, P]), s["ident"][:], start=True, stop=True)
            mat(mm)
            pe.wait_ge(vec.sem, at["ptr"])
            nc.tensor.matmul(ps[:, 1, 0:NB], sh1[:], ptr[:, 0:NB], start=True, stop=False)
            mat(nc.tensor.matmul(ps[:, 1, 0:NB], sh2[:], ptr[:, 1:NB + 1], start=False, stop=True))
            pe.wait_ge(vec.sem, at["cum", NB - 1])
            mat(nc.tensor.matmul(ps[:, 0, 0:P], oneb[:], cum[:, NB, :], start=True, stop=True))
            for g in range(-(-NB // 4)):
                if g >= 2:
                    pe.wait_ge(vec.sem, at["pre", g - 2])
                for j in range(min(4, NB - 4 * g)):
                    b = 4 * g + j
                    nc.tensor.matmul(ps[:, 2 + g % 2, j * P:(j + 1) * P], oneb[:], cum[:, b, :], start=True, stop=False)
                    last = nc.tensor.matmul(ps[:, 2 + g % 2, j * P:(j + 1) * P], ltri[:], oh[:, b, :], start=False, stop=True)
                mat(last)

        @block.scalar
        def _(a):
            a.wait_ge(ld_edge, 16 * 8)
            a.wait_ge(vec.sem, at["reduced"])
            for q in range(NQ):
                if q >= 2:
                    a.wait_ge(rows_out[q % 2], 16 * (q // 2))
                o = rowq[:, q % 2, :, :].rearrange("p e (j c) -> p e j c", c=REC)

                def span(tile, width, c, n):
                    return bass.AP(tensor=tile[:].tensor, offset=q * Q * width + c,
                                   ap=[[W * width, P], [width, Q], [width, CH], [1, n]])
                nc.scalar.activation(o[:, :, :, 0:1], span(srci, 1, 0, 1), ACT.Copy)
                nc.scalar.activation(o[:, :, :, 1:2], span(wgt, 1, 0, 1), ACT.Copy)
                nc.scalar.activation(o[:, :, :, 2:3], span(at2, 2, 0, 1), ACT.Copy)
                nc.scalar.activation(o[:, :, :, 3:8], span(at5, 5, 0, 5), ACT.Copy).then_inc(piece, 1)

        @block.sync
        def _(sp):
            sp.wait_ge(vec.sem, at["pad_dst"])
            sp.dma_start(dsti[0:P - 1, :], bass.AP(tensor=dst.tensor, offset=0, ap=[[EC, P - 1], [1, EC]])).then_inc(ld_dst, 16)
            sp.dma_start(dsti[P - 1:P, 0:ELAST], bass.AP(tensor=dst.tensor, offset=(P - 1) * EC, ap=[[ELAST, 1], [1, ELAST]])).then_inc(ld_dst, 16)
            sp.wait_ge(pads, 4)
            for a, tile, wd in ((src, srci[:], 1), (ew, wgt[:], 1), (ea2, at2[:].rearrange("p a b -> p (a b)"), 2),
                                (ea5, at5[:].rearrange("p a b -> p (a b)"), 5)):
                sp.dma_start(tile[0:P - 1, :], overlapped(a, wd)).then_inc(ld_edge, 16)
                sp.dma_start(tile[P - 1:P, 0:ELAST * wd], bass.AP(tensor=a.tensor, offset=(P - 1) * EC * wd, ap=[[ELAST * wd, 1], [1, ELAST * wd]])).then_inc(ld_edge, 16)
            sp.wait_ge(vec.sem, at["dstr"])
            sp.dma_start(t["dstf"].rearrange("(p r) e -> p (r e)", r=RUNS), dstr[:]).then_inc(dst_out, 16)
            whole = N // P
            sp.wait_ge(vec.sem, at["pad_x"])
            sp.dma_start(info[:, 0:whole, 0:D], x[0:whole * P, :].rearrange("(b p) d -> p b d", p=P)).then_inc(x_in, 16)
            sp.dma_start(info[0:N - whole * P, whole, 0:D], x[whole * P:N, :]).then_inc(x_in, 16)
            recs = t["recs"].rearrange("(p e) w -> p e w", p=P)
            for q in range(NQ):
                sp.wait_ge(piece, q + 1)
                sp.dma_start(recs[:, q * Q:(q + 1) * Q, :], rowq[:, q % 2, :, :]).then_inc(rows_out[q % 2], 16)
            sp.wait_ge(sorted_out, 16 * NB)
            back = t["info"].rearrange("(b p) c -> p b c", p=P)
            sp.dma_start(infp[:], back[:, :, D:D + 4]).then_inc(info_in, 16)
            sp.dma_start(s["xp"][:, 0:NB, :], back[:, :, 0:D]).then_inc(info_in, 16)
            sp.wait_ge(info_in, 32)
            sp.wait_ge(rows_out[0], 16 * (-(-NQ // 2)))
            sp.wait_ge(rows_out[1], 16 * (NQ // 2))


def chunk_tables(nc, t, s):
    with ExitStack() as ctx:
        def sb(name, shape, dt=F32):
            return ctx.enter_context(nc.sbuf_tensor(name, shape, dt))

        def sem(name):
            return nc.alloc_semaphore(name)

        ptrT = sb("ptrT", [NB, P])
        degT = sb("degT", [NB, P])
        smax = sb("smax", [NB, 1])
        nch = sb("nch", [NB, 1])
        lowtri = sb("lowtri", [NB, NB])
        fi = sb("iota_f", [NB, SLAB])
        pi = sb("iota_p", [NB, 1])
        pib = sb("blk_less_nb", [NB, P])
        chs = sb("ch_rows", [NB, P])
        mch = sb("minus_ch_rows", [NB, P])
        first = sb("first", [NB, 1])
        after = sb("after", [NB, 1])
        cf = sb("cnt_f", [1, 4])
        cio = sb("chunk_no", [NB, SLAB])
        ge = sb("ge", [NB, SLAB])
        one = sb("one_hot", [NB, SLAB])
        jj = sb("chunk_of_block", [NB, SLAB])
        tab = sb("tab", [P, SLAB, 4], I32)
        lim = sb("lim_part", [P, SLAB])
        blk = sb("blk", [1, SLAB], I32)
        lead = sb("lead", [1, 4], I32)
        ps = ctx.enter_context(nc.psum_tensor("ps_tab", [P, 6, 512], F32))
        tabf = tab[:].bitcast(F32)

        iotas = sem("tab_iotas")
        vec = Tick(sem("tab_vec"))
        mat = Tick(sem("tab_mat"))
        slab_v = sem("slab_vec")
        slab_ready = sem("slab_ready")
        slab_mat = sem("slab_mat")
        slab_hot = sem("slab_hot")
        slab_out = sem("slab_out")
        at = {}
        block = ctx.enter_context(nc.Block())
        VS = 9

        @block.vector
        def _(v):
            def do(ins, key=None):
                n = vec(ins)
                v.wait_ge(vec.sem, n)
                if key:
                    at[key] = n

            v.wait_ge(mat.sem, 2)
            do(nc.vector.tensor_copy(ptrT[:], ps[0:NB, 0, 0:P]))
            do(nc.vector.tensor_copy(degT[:], ps[0:NB, 1, 0:P]))
            do(nc.vector.tensor_reduce(smax[:], degT[:], AX.X, ALU.max))
            do(nc.vector.tensor_scalar(nch[:], smax[:], CH - 1.0, 1.0 / CH, ALU.add, ALU.mult))
            do(nc.vector.tensor_scalar(nch[:], nch[:], 0.5 - 0.5 / CH, 8388608.0, ALU.subtract, ALU.add))
            do(nc.vector.tensor_scalar(nch[:], nch[:], 8388608.0, None, ALU.subtract))
            v.wait_ge(iotas, 2)
            do(nc.vector.tensor_scalar(lowtri[:], fi[:, 0:NB], pi[:, 0:1], None, ALU.is_gt))
            do(nc.vector.memset(chs[:], float(CH)))
            do(nc.vector.memset(mch[:], -float(CH)))
            do(nc.vector.memset(lead[:], NB - 1))
            do(nc.vector.tensor_scalar(pib[:], s["ones"][0:NB, :], pi[:, 0:1], NB - 1.0, ALU.mult, ALU.subtract), "first_in")
            v.wait_ge(mat.sem, 3)
            do(nc.vector.tensor_copy(first[:], ps[0:NB, 2, 0:1]))
            do(nc.vector.tensor_tensor(after[:], first[:], nch[:], ALU.add))
            do(nc.vector.tensor_scalar(cf[:, 0:1], ps[0:1, 3, 0:1], U - 1.0 + LEAD, 1.0 / U, ALU.add, ALU.mult))
            do(nc.vector.tensor_scalar(cf[:, 1:2], ps[0:1, 3, 0:1], 3.0 * U, 1.0 / SLAB, ALU.add, ALU.mult))
            do(nc.vector.tensor_scalar(cf[:, 0:1], cf[:, 0:1], 0.5 - 0.5 / U, 8388608.0, ALU.subtract, ALU.add))
            do(nc.vector.tensor_scalar(cf[:, 1:2], cf[:, 1:2], 0.5 - 0.5 / SLAB, 8388608.0, ALU.subtract, ALU.add))
            do(nc.vector.tensor_scalar(cf[:, 0:1], cf[:, 0:1], 8388608.0, None, ALU.subtract))
            do(nc.vector.tensor_scalar(cf[:, 1:2], cf[:, 1:2], 8388608.0 - 1.0, None, ALU.subtract))
            do(nc.vector.memset(s["cnt"][:], 0))
            do(nc.vector.tensor_copy(s["cnt"][:, 0:2], cf[:, 0:2]))
            do(nc.vector.tensor_copy(cio[:], fi[:]), "counts")
            slabs = v.value_load(s["cnt"][0:1, 1:2], min_val=1, max_val=SLABS)
            with v.Fori(0, slabs) as k:
                def step(ins, n):
                    ins.then_inc(slab_v, 1)
                    v.wait_ge(slab_v, k * VS + n)

                step(nc.vector.tensor_scalar(ge[:], cio[:], first[:, 0:1], None, ALU.is_ge), 1)
                step(nc.vector.scalar_tensor_tensor(one[:], cio[:], after[:, 0:1], ge[:], ALU.is_lt, ALU.mult), 2)
                nc.vector.scalar_tensor_tensor(jj[:], cio[:], first[:, 0:1], one[:], ALU.subtract, ALU.mult).then_inc(slab_hot, 1)
                v.wait_ge(slab_hot, k + 1)
                step(nc.vector.tensor_scalar(cio[:], cio[:], float(SLAB), None, ALU.add), 3)
                v.wait_ge(slab_mat, k + 1)
                v.wait_ge(slab_out, k * 32 + 16)
                step(nc.vector.tensor_scalar(tab[:, :, 0], ps[:, 0, :], E - 1.0, None, ALU.min), 4)
                step(nc.vector.tensor_copy(tabf[:, :, 1], ps[:, 1, :]), 5)
                step(nc.vector.tensor_scalar(lim[:], ps[:, 2, :], 0.5, RESET, ALU.is_lt, ALU.mult), 6)
                step(nc.vector.tensor_scalar(tabf[:, :, 3], ps[:, 2, :], 0.5, None, ALU.is_gt), 7)
                step(nc.vector.tensor_scalar(tabf[:, :, 2], tabf[:, :, 3], HUGE, None, ALU.mult), 8)
                step(nc.vector.tensor_tensor(tabf[:, :, 2], tabf[:, :, 2], lim[:], ALU.add), 9)
                nc.vector.tensor_scalar(blk[:], ps[0:1, 3, :], NB - 1.0, None, ALU.add).then_inc(slab_ready, 1)

        @block.gpsimd
        def _(p):
            nc.gpsimd.iota(fi[:], [[1, SLAB]], base=0, channel_multiplier=0, allow_small_or_imprecise_dtypes=True).then_inc(iotas, 1)
            nc.gpsimd.iota(pi[:], [[1, 1]], base=0, channel_multiplier=1, allow_small_or_imprecise_dtypes=True).then_inc(iotas, 1)

            p.wait_ge(vec.sem, at["counts"])
            slabs = p.value_load(s["cnt"][0:1, 1:2], min_val=1, max_val=SLABS)
            p.wait_ge(slab_out, slabs * 32 + 16)

        @block.tensor
        def _(pe):
            mat(nc.tensor.transpose(ps[0:NB, 0, 0:P], s["ptrp"][:], s["ident"][:]))
            mat(nc.tensor.transpose(ps[0:NB, 1, 0:P], s["degp"][:], s["ident"][:]))
            pe.wait_ge(vec.sem, at["first_in"])
            nc.tensor.matmul(ps[0:NB, 2, 0:1], lowtri[:], nch[:], start=True, stop=True)
            mat(nc.tensor.matmul(ps[0:1, 3, 0:1], s["ones"][0:NB, 0:1], nch[:], start=True, stop=True))
            pe.wait_ge(vec.sem, at["counts"])
            slabs = pe.value_load(s["cnt"][0:1, 1:2], min_val=1, max_val=SLABS)
            with pe.Fori(0, slabs) as k:
                pe.wait_ge(slab_hot, k + 1)
                pe.wait_ge(slab_v, k * VS + 2)
                nc.tensor.matmul(ps[:, 0, :], ptrT[:], one[:], start=True, stop=False)
                nc.tensor.matmul(ps[:, 0, :], chs[:], jj[:], start=False, stop=True)
                nc.tensor.matmul(ps[:, 1, :], degT[:], one[:], start=True, stop=False)
                nc.tensor.matmul(ps[:, 1, :], mch[:], jj[:], start=False, stop=True)
                nc.tensor.matmul(ps[:, 2, :], s["ones"][0:NB, :], jj[:], start=True, stop=True)
                nc.tensor.matmul(ps[:, 3, :], pib[:], one[:], start=True, stop=True).then_inc(slab_mat, 1)

        @block.sync
        def _(sp):
            sp.wait_ge(vec.sem, at["counts"])
            sp.dma_start(t["blk"][:, 0:LEAD], lead[:, 0:LEAD]).then_inc(slab_out, 16)
            sp.wait_ge(slab_out, 16)
            slabs = sp.value_load(s["cnt"][0:1, 1:2], min_val=1, max_val=SLABS)
            with sp.Fori(0, slabs) as k:
                to_tab = sp.snap(k * (4 * SLAB))
                to_blk = sp.snap(k * SLAB + LEAD)
                sp.wait_ge(slab_ready, k + 1)
                sp.dma_start(t["tab"][:, bass.ds(to_tab, 4 * SLAB)], tab[:].rearrange("p c w -> p (c w)")).then_inc(slab_out, 16)
                sp.dma_start(t["blk"][:, bass.ds(to_blk, SLAB)], blk[:]).then_inc(slab_out, 16)


def row_stats(nc, v, st6, mv, done, width):
    def step(ins, n):
        ins.then_inc(done, 1)
        v.wait_ge(done, n)

    step(nc.vector.tensor_tensor(mv[:, :, 0], st6[:, :, 1], st6[:, :, 4], ALU.add), 1)
    step(nc.vector.tensor_tensor(mv[:, :, 1], st6[:, :, 1], st6[:, :, 4], ALU.subtract), 2)
    step(nc.vector.tensor_tensor(mv[:, :, 1], mv[:, :, 1], mv[:, :, 1], ALU.mult), 3)
    step(nc.vector.tensor_tensor(st6[:, :, 2], st6[:, :, 2], st6[:, :, 5], ALU.add), 4)
    nc.vector.tensor_scalar(mv[:, :, 0], mv[:, :, 0], 0.5, None, ALU.mult)
    nc.vector.tensor_scalar(mv[:, :, 1], mv[:, :, 1], 0.25, None, ALU.mult)
    step(nc.vector.tensor_scalar(st6[:, :, 2], st6[:, :, 2], 1.0 / width, None, ALU.mult), 5)
    step(nc.vector.tensor_tensor(mv[:, :, 1], mv[:, :, 1], st6[:, :, 2], ALU.add), 6)


def project_rows(nc, t, s, layer, w):
    with ExitStack() as ctx:
        def sb(name, shape, dt=F32):
            return ctx.enter_context(nc.sbuf_tensor(f"{name}_{layer}", shape, dt))

        def sem(name):
            return nc.alloc_semaphore(f"{name}_{layer}")

        heads = H0 if layer == 0 else H2
        hk = D // heads
        cols = {0: 3 * D + H0, 2: 2 * D + H2, 3: D + 2 * H2}[layer]
        row_w = ROW0 if layer == 0 else ROW2
        rhs = sb("rhs", [P, cols])
        bias = sb("bias", [P, cols])
        st6 = sb("st6", [P, NBX, 6])
        mv = sb("mv", [P, NBX, 2])
        rstd = sb("rstd", [P, NBX])
        hT = sb("hT", [P, 2, P])
        RR = 5
        UN = 2 * RR
        rows = sb("rows", [P, RR, row_w])
        idx = sb("idx", [P, RR], I32)
        hp = sb("head_of", [P, heads])
        hmask = sb("head_mask", [P, heads])
        credit = sb("credit", [P, 4 * RR])
        xn = sb("xn", [P, 2, D])
        ps_t = ctx.enter_context(nc.psum_tensor(f"ps_t_{layer}", [P, 2, 512], F32))
        ps_r = ctx.enter_context(nc.psum_tensor(f"ps_r_{layer}", [P, 2, 512], F32))
        ps_w = ctx.enter_context(nc.psum_tensor(f"ps_w_{layer}", [P, 512], F32))
        nat = sb("nat", [P, 2, D])
        mix = sb("mix", [P, D])
        col = sb("col", [P, 4])
        rb = sb("rb", [P, 2 * heads])
        wtmp = sb("wtmp", [P, D])

        ld = sem("w_in")
        iotas = sem("w_iota")
        vec = Tick(sem("w_vec"))
        mat = Tick(sem("w_mat"))
        stats1, stats2, var_ok = sem("stats1"), sem("stats2"), sem("sqrt_done")
        turned, h_ready, product = sem("turned"), sem("h_ready"), sem("product")
        row_ready, evacuated = sem("row_ready"), sem("evacuated")
        xn_ready = sem("xn_ready")
        cleared = sem("mix_cleared")
        passed = sem("passed")
        row_out = [sem(f"row_out{u}") for u in range(RR)]
        at = {}
        ld_n = [0]
        block = ctx.enter_context(nc.Block())

        @block.sync
        def _(sp):
            def load(o, i):
                sp.dma_start(o, i).then_inc(ld, 16)
                ld_n[0] += 16

            def spread(a):
                return bass.AP(tensor=a.tensor, offset=0, ap=[[0, P], [1, D]])

            if layer == 0:
                load(rhs[:, 0:D], w["L0_gnn_WkT"])
                load(wtmp[:], w["L0_gnn_WqT"])
                load(nat[:, 0, :], w["L0_gnn_Wk"])
                load(nat[:, 1, :], w["L0_gnn_Wv"])
                load(bias[:, 0:D], spread(w["L0_gnn_bk"]))
                load(bias[:, 2 * D + H0:], spread(w["L0_gnn_bq"]))
                load(col[:, 0:1], w["L0_gnn_rel_att"].rearrange("h (d a) -> (h d) a", a=1))
                load(col[:, 1:2], w["L0_gnn_bk"].rearrange("(d a) -> d a", a=1))
                load(col[:, 2:3], w["L0_gnn_bv"].rearrange("(d a) -> d a", a=1))
                sp.wait_ge(cleared, 1)
                for h in range(H0):
                    load(mix[h * K0:(h + 1) * K0, h * K0:(h + 1) * K0], w["L0_gnn_rel_msg"][h])
            elif layer == 2:
                load(rhs[:, 0:D], w["L2_gnn_W_linT"])
                load(rhs[:, D + H2:], w["L2_gnn_W_resT"])
                load(nat[:, 0, :], w["L2_gnn_W_lin"])
                load(col[:, 0:1], w["L2_gnn_att"].rearrange("h (d a) -> (h d) a", a=1))
            else:
                load(rhs[:, 0:D], w["L3_gnn_weight"].rearrange("i h o -> i (h o)"))
                load(nat[:, 0, :], w["L3_gnn_weightT"])
                for half in range(2):
                    for h in range(H2):
                        load(col[h * K2:(h + 1) * K2, half:half + 1],
                             w["L3_gnn_att_weight"][h:h + 1, half * K2:(half + 1) * K2].rearrange("a d -> d a"))

        @block.vector
        def _(v):
            def do(ins, key=None):
                n = vec(ins)
                v.wait_ge(vec.sem, n)
                if key:
                    at[key] = n

            if layer == 0:
                nc.vector.memset(mix[:], 0.0).then_inc(cleared, 1)
            with v.Fori(0, NBX // 13) as i:
                for u in range(13):
                    b = i * 13 + u
                    nc.vector.bn_stats(flat(st6[:, bass.ds(b, 1), :]), flat(s["xp"][:, bass.ds(b, 1), :])).then_inc(stats1, 1)
            v.wait_ge(stats1, NBX)
            row_stats(nc, v, st6, mv, stats2, D)
            v.wait_ge(iotas, 1)
            do(nc.vector.tensor_scalar(hmask[:], hp[:], -0.5, None, ALU.is_gt))
            do(nc.vector.scalar_tensor_tensor(hmask[:], hp[:], hk - 0.5, hmask[:], ALU.is_lt, ALU.mult))
            v.wait_ge(ld, ld_n[0])
            if layer == 0:
                do(nc.vector.tensor_scalar(rb[:, 0:heads], hmask[:], col[:, 0:1], 0.25, ALU.mult, ALU.mult))
                do(nc.vector.tensor_scalar(rhs[:, 2 * D + H0:], wtmp[:], 0.25, None, ALU.mult))
                do(nc.vector.tensor_scalar(bias[:, 2 * D + H0:], bias[:, 2 * D + H0:], 0.25, None, ALU.mult), "w0")
                v.wait_ge(mat.sem, 1)
                do(nc.vector.tensor_copy(rhs[:, D:2 * D + H0], ps_w[:, 0:D + H0]))
                do(nc.vector.tensor_copy(bias[:, D:2 * D + H0], ps_w[:, D + H0:2 * (D + H0)]), "w1")
                v.wait_ge(vec.sem, vec.n)
                for u in range(RR):
                    do(nc.vector.memset(rows[:, u, D + H0:].rearrange("p (h k) -> p h k", h=H0)[:, :, K0:], 1.0))
            elif layer == 2:
                do(nc.vector.tensor_scalar(rb[:, 0:heads], hmask[:], col[:, 0:1], 0.6, ALU.mult, ALU.mult), "w0")
                v.wait_ge(mat.sem, 1)
                do(nc.vector.tensor_copy(rhs[:, D:D + H2], ps_w[:, 0:H2]), "w1")
            else:
                do(nc.vector.tensor_scalar(rb[:, 0:heads], hmask[:], col[:, 0:1], None, ALU.mult))
                do(nc.vector.tensor_scalar(rb[:, heads:], hmask[:], col[:, 1:2], None, ALU.mult), "w0")
                v.wait_ge(mat.sem, 1)
                do(nc.vector.tensor_copy(rhs[:, D:D + 2 * H2], ps_w[:, 0:2 * H2]), "w1")
            if layer != 0:
                for u in range(RR):
                    do(nc.vector.memset(rows[:, u, 0:V2].rearrange("p (h k) -> p h k", h=H2)[:, :, K2:], 1.0))
            v.wait_ge(var_ok, 1)
            do(nc.vector.reciprocal(rstd[:], rstd[:]))

            def normalise(b, u):
                nc.vector.tensor_scalar(xn[:, u, :], s["xp"][:, bass.ds(b, 1), :].rearrange("p a b -> p (a b)"),
                                        mv[:, bass.ds(b, 1), 0:1].rearrange("p a b -> p (a b)"),
                                        rstd[:, bass.ds(b, 1)], ALU.subtract, ALU.mult).then_inc(xn_ready, 1)

            normalise(0, 0)
            normalise(1, 1)
            v.sem_inc(evacuated, 2)
            v.sem_inc(product, 2)
            with v.Fori(0, NB // UN) as i:
                for u in range(UN):
                    b = i * UN + u
                    m, q = u % 2, u % RR
                    v.wait_ge(turned, b + 1)
                    normalise(b + 2, m)
                    v.wait_ge(product, b + 3)
                    v.wait_ge(row_out[q], i * 32 + (16 if u < RR else 32))
                    r, pr = rows[:, q, :], ps_r[:, m, :]
                    nc.vector.tensor_copy(idx[:, q:q + 1], s["nid"][:, bass.ds(b, 1)])
                    if layer == 0:
                        nc.vector.tensor_tensor(r[:, 0:D + H0], pr[:, 0:D + H0], bias[:, 0:D + H0], ALU.add)
                        nc.vector.tensor_tensor(
                            r[:, D + H0:].rearrange("p (h k) -> p h k", h=H0)[:, :, 0:K0],
                            pr[:, D + H0:2 * D + H0].rearrange("p (h k) -> p h k", h=H0),
                            bias[:, D + H0:2 * D + H0].rearrange("p (h k) -> p h k", h=H0), ALU.add).then_inc(row_ready, 1)
                        nc.vector.tensor_tensor(s["tgt"][:, bass.ds(b, 1), :].rearrange("p a b -> p (a b)"),
                                                pr[:, 2 * D + H0:3 * D + H0], bias[:, 2 * D + H0:], ALU.add).then_inc(evacuated, 1)
                        continue
                    vals = r[:, 0:V2].rearrange("p (h k) -> p h k", h=H2)[:, :, 0:K2]
                    nc.vector.tensor_copy(vals, pr[:, 0:D].rearrange("p (h k) -> p h k", h=H2))
                    if layer == 2:
                        nc.vector.tensor_copy(r[:, V2:], pr[:, D:D + H2]).then_inc(row_ready, 1)
                        nc.vector.tensor_copy(s["tgt"][:, bass.ds(b, 1), :].rearrange("p a b -> p (a b)"), pr[:, 0:D])
                        nc.vector.tensor_copy(s["tsc"][:, bass.ds(b, 1), :].rearrange("p a b -> p (a b)"), pr[:, D:D + H2])
                        nc.vector.tensor_tensor(s["xp"][:, bass.ds(b, 1), :].rearrange("p a b -> p (a b)"),
                                                s["xp"][:, bass.ds(b, 1), :].rearrange("p a b -> p (a b)"),
                                                pr[:, D + H2:cols], ALU.add).then_inc(evacuated, 1)
                    else:
                        nc.vector.tensor_copy(r[:, V2:], pr[:, D + H2:D + 2 * H2]).then_inc(row_ready, 1)
                        nc.vector.tensor_copy(s["tsc"][:, bass.ds(b, 1), :].rearrange("p a b -> p (a b)"),
                                              pr[:, D:D + H2]).then_inc(evacuated, 1)

        @block.scalar
        def _(a):
            a.wait_ge(vec.sem, at["w0"])
            a.wait_ge(stats2, 6)
            nc.scalar.activation(rstd[:], mv[:, :, 1], ACT.Sqrt, bias=s["eps"][:, 0:1]).then_inc(var_ok, 1)
            with a.Fori(0, NB // UN) as i:
                for u in range(UN):
                    m = u % 2
                    a.wait_ge(turned, i * UN + u + 1)
                    a.wait_ge(product, i * UN + u + 1)
                    nc.scalar.activation(hT[:, m, :], ps_t[:, m, 0:P], ACT.Relu).then_inc(h_ready, 1)

        @block.tensor
        def _(pe):
            pe.wait_ge(vec.sem, at["w0"])
            if layer == 0:
                nc.tensor.matmul(ps_w[:, 0:H0], nat[:, 0, :], rb[:, 0:H0], start=True, stop=True)
                nc.tensor.matmul(ps_w[:, H0:D + H0], nat[:, 1, :], mix[:], start=True, stop=True)
                o = D + H0
                nc.tensor.matmul(ps_w[:, o:o + H0], col[:, 1:2].to_broadcast([P, P]), rb[:, 0:H0], start=True, stop=True)
                mat(nc.tensor.matmul(ps_w[:, o + H0:o + H0 + D], col[:, 2:3].to_broadcast([P, P]), mix[:], start=True, stop=True))
            elif layer == 2:
                mat(nc.tensor.matmul(ps_w[:, 0:H2], nat[:, 0, :], rb[:, 0:H2], start=True, stop=True))
            else:
                mat(nc.tensor.matmul(ps_w[:, 0:2 * H2], nat[:, 0, :], rb[:], start=True, stop=True))
            pe.wait_ge(vec.sem, at["w1"])

            def turn(b, u):
                pe.wait_ge(xn_ready, b + 1)
                nc.tensor.transpose(ps_t[:, u, 0:P], xn[:, u, :], s["ident"][:]).then_inc(turned, 1)

            turn(0, 0)
            turn(1, 1)
            with pe.Fori(0, NB // UN) as i:
                for u in range(UN):
                    b = i * UN + u
                    m = u % 2
                    pe.wait_ge(h_ready, b + 1)
                    pe.wait_ge(evacuated, b + 1)
                    nc.tensor.matmul(ps_r[:, m, 0:cols], hT[:, m, :], rhs[:], start=True, stop=True).then_inc(product, 1)
                    turn(b + 2, m)

        @block.gpsimd
        def _(p):
            nc.gpsimd.iota(hp[:], [[-hk, heads]], base=0, channel_multiplier=1, allow_small_or_imprecise_dtypes=True).then_inc(iotas, 1)
            for u in range(RR):
                p.dma_start(credit[:, 4 * u:4 * u + 4], t["info"][0:P, D:D + 4]).then_inc(row_out[u], 16)
            with p.Fori(0, NB // UN) as i:
                for u in range(UN):
                    q = u % RR
                    p.wait_ge(row_ready, i * UN + u + 1)
                    p.sem_inc(passed, 1)
                    nc.gpsimd.indirect_dma_start(out=t[f"row{layer}"], out_offset=bass.IndirectOffsetOnAxis(ap=idx[:, q:q + 1], axis=0),
                                                 in_=rows[:, q, :], in_offset=None).then_inc(row_out[q], 16)
            for q in range(RR):
                p.wait_ge(row_out[q], 16 + 16 * (NB // RR))


def block_numbers(nc, engine, t, i, n, first):
    _, values = nc.values_load_multi_w_load_instructions(
        t["blk"][0:1, bass.ds(i * U + (LEAD + first), n)], engines=(engine,), min_val=0, max_val=NB - 1,
        skip_runtime_bounds_check_because="the table was made on this chip from comparisons with the blocks' first chunks")
    return values


def flat(ap):
    return ap.rearrange("p a b -> p (a b)")


def edges_layer0(nc, t, s, w):
    with ExitStack() as ctx:
        def sb(name, shape, dt=F32):
            return ctx.enter_context(nc.sbuf_tensor(f"{name}_e0", shape, dt))

        def sem(name):
            return nc.alloc_semaphore(f"{name}_e0")

        R = 4
        assert R == U
        assert V0 == ROW2
        HID = CH * P
        tab = sb("tab", [P, R, 4], I32)
        rec = sb("rec", [P, R, GROW])
        meta = sb("meta", [P, R, 2 * CH], I32)
        lk = sb("lim_keep", [P, R, 2])
        vbias = sb("vbias", [P, R, CH])
        xm = sb("xm", [P, R, CH, 6])
        gat = sb("gathered", [P, R, CH + 1, ROW0])
        prod = sb("prod", [P, CH, H0, K0 + 2])
        att = sb("att", [P, CH + 2, H0])
        top = sb("top", [P, H0])
        dif = sb("dif", [P, R, CH + 1, H0])
        exps = sb("exps", [P, R, CH + 1, H0])
        wv = sb("wv", [P, CH + 1, V0])
        io = sb("slot_no", [P, CH])
        xT = sb("xT", [MX, R, P])
        h1 = sb("h1", [P, 2, HID])
        h2 = sb("h2", [P, 2, HID])
        w1x = sb("w1x", [MX, CH, P])
        w2x = sb("w2x", [MX, CH, P])
        w2T = sb("w2T", [P, P])
        w3T = sb("w3T", [P, P])
        w1b = sb("w1b", [MX, P])
        w1n = sb("w1n", [P, CH, 6])
        b2r = sb("b2r", [1, P])
        vrow = sb("vrow", [1, MX])
        smask = sb("smask", [MX, CH])
        sio = sb("sio", [MX, CH])
        b2m = sb("b2m", [MX, P])
        last = s["acc"]
        msg = s["msg"]
        ps_x = ctx.enter_context(nc.psum_tensor("ps_x", [P, 512], F32))
        ps_1 = ctx.enter_context(nc.psum_tensor("ps_1", [P, 1024], F32))
        ps_2 = ctx.enter_context(nc.psum_tensor("ps_2", [P, 2, 1024], F32))
        ps_3 = ctx.enter_context(nc.psum_tensor("ps_3", [P, 512], F32))

        tab_in = [sem(f"tab_in{u}") for u in range(R)]
        rec_in = [sem(f"rec_in{u}") for u in range(R)]
        rows_in = [sem(f"rows_in{u}") for u in range(R)]
        meta_out = [sem(f"meta_out{u}") for u in range(R)]
        passed = sem("passed")
        w_in, iotas, zeroed = sem("w_in"), sem("iotas"), sem("zeroed")
        vec, mat = Tick(sem("w_vec")), Tick(sem("w_mat"))
        idx_ready, valid_ready, masks_ready = sem("idx_ready"), sem("valid_ready"), sem("masks_ready")
        summed, leaky_done = sem("messages_summed"), sem("leaky_done")
        prods, logits, maxed, dif_ready = sem("prods"), sem("logits"), sem("maxed"), sem("dif_ready")
        weighted, acc_ready = sem("weighted"), sem("acc_ready")
        relu2_done, relu1_done, xT_ready, exps_ready, acc_kept = (sem(n) for n in (
            "relu2_done", "relu1_done", "xT_ready", "exps_ready", "acc_kept"))
        m3_done, m2_done, m1_done, x_turned = sem("m3_done"), sem("m2_done"), sem("m1_done"), sem("x_turned")
        at = {}
        block = ctx.enter_context(nc.Block())

        at["w_in"] = 16 * (2 * CH + 5)

        @block.vector
        def _(v):
            def do(ins, key=None):
                n = vec(ins)
                v.wait_ge(vec.sem, n)
                if key:
                    at[key] = n

            for tile in (ps_x, ps_1, ps_2, ps_3, h1, h2, xT, att, top, exps, prod, lk, meta):
                do(nc.vector.memset(tile[:], 0.0))
            do(nc.vector.memset(att[:, CH + 1, :], FLOOR))
            do(nc.vector.memset(w1n[:], 0.0))
            do(nc.vector.memset(vrow[:], 0.0))
            do(nc.vector.memset(vrow[:].rearrange("p (s c) -> p s c", c=6)[:, :, 5:6], 1.0), "cleared")
            v.wait_ge(iotas, 2)
            do(nc.vector.tensor_scalar(smask[:], sio[:], -0.5, None, ALU.is_gt))
            do(nc.vector.scalar_tensor_tensor(smask[:], sio[:], 5.5, smask[:], ALU.is_lt, ALU.mult))
            v.wait_ge(w_in, at["w_in"])
            do(nc.vector.tensor_scalar(w1n[:, 0:1, :].rearrange("p a b -> p (a b)"), w1n[:, 0:1, :].rearrange("p a b -> p (a b)"), 0.01, None, ALU.mult))
            for k in range(1, CH):
                do(nc.vector.tensor_copy(w1n[:, k, :], w1n[:, 0, :]), "w1n")
            for k in range(CH):
                do(nc.vector.tensor_scalar(w1x[:, k, :], w1b[:], smask[:, k:k + 1], None, ALU.mult))
            v.wait_ge(mat.sem, 1)
            do(nc.vector.tensor_copy(b2m[:], ps_3[0:MX, 0:P]))
            do(nc.vector.tensor_tensor(b2m[:], b2m[:], ps_3[0:MX, P:2 * P], ALU.add))
            for k in range(CH):
                do(nc.vector.tensor_scalar(w2x[:, k, :], b2m[:], smask[:, k:k + 1], None, ALU.mult))
            for ring, k in ((prods, 2), (weighted, 3), (m3_done, 1), (x_turned, 3), (relu2_done, 1), (exps_ready, 1),
                            (relu1_done, 1), (acc_kept, 1)):
                v.sem_inc(ring, k)
            v.wait_ge(zeroed, 3)
            at["weights"] = vec.n

            def indices(m):
                r = rec[:, m, :].rearrange("p (s c) -> p s c", c=REC)
                nc.vector.tensor_copy(meta[:, m, 0:CH], r[:, :, 0]).then_inc(idx_ready, 1)

            def masks(c, m, sums=None):
                r = rec[:, m, :].rearrange("p (s c) -> p s c", c=REC)
                left = tab[:].bitcast(F32)[:, m, 1:2]
                nc.vector.tensor_scalar(xm[:, m, :, 5], io[:], left, None, ALU.is_lt).then_inc(valid_ready, 1)
                nc.vector.tensor_copy(meta[:].bitcast(F32)[:, m, CH:2 * CH], r[:, :, 2])
                nc.vector.tensor_scalar(vbias[:, m, :], io[:], left, -BIG, ALU.is_ge, ALU.mult)
                if sums is not None:
                    v.wait_ge(summed, sums)
                nc.vector.tensor_copy(lk[:, m, :], tab[:].bitcast(F32)[:, m, 2:4])
                v.wait_ge(valid_ready, c + 1)
                nc.vector.tensor_tensor(xm[:, m, :, 0:5], r[:, :, 3:8], xm[:, m, :, 5:6].to_broadcast([P, CH, 5]),
                                        ALU.mult).then_inc(masks_ready, 1)

            for m in range(2):
                v.wait_ge(rec_in[m], 16)
                indices(m)
            masks(0, 0)
            iters = v.value_load(s["cnt"][0:1, 0:1], min_val=1, max_val=NCMAX // U - 2)
            with v.Fori(0, iters) as i:
                blks = block_numbers(nc, v.engine, t, i, U + 3, -3)
                for u in range(U):
                    c = i * U + u
                    m = (u + 1) % R
                    v.wait_ge(m3_done, c + 1)
                    mt = flat(msg[:, bass.ds(blks[u], 1), :])
                    nc.vector.scalar_tensor_tensor(mt, mt, lk[:, m, 1:2], ps_3[:, 0:P], ALU.mult, ALU.add).then_inc(summed, 1)
                    n = (u + 2) % R
                    v.wait_ge(rec_in[n], i * 16 + (16 if u < R - 2 else 32))
                    v.wait_ge(meta_out[n], i * 16 + (16 if u < R - 2 else 32))
                    indices(n)
                    v.wait_ge(x_turned, c + 1)
                    masks(c + 1, m, c + 1)
                    v.wait_ge(relu2_done, c + 1)
                    hh = h2[:, u % 2, :]
                    nc.vector.scalar_tensor_tensor(hh, ps_2[:, u % 2, 0:HID], 0.01, hh, ALU.mult, ALU.add).then_inc(leaky_done, 1)
                    v.wait_ge(rows_in[u], i * (16 * CH) + 16 * CH)
                    g = gat[:, u, 1:CH + 1, :]
                    k = g[:, :, 0:D].rearrange("p s (h k) -> p s h k", h=H0)
                    q = flat(s["tgt"][:, bass.ds(blks[u + 3], 1), :]).rearrange("p (h k) -> p h k", h=H0)
                    nc.vector.tensor_tensor(prod[:, :, :, 0:K0], k, q.unsqueeze(1).to_broadcast([P, CH, H0, K0]), ALU.mult)
                    ew = rec[:, u, :].rearrange("p (s c) -> p s c", c=REC)[:, :, 1:2]
                    nc.vector.tensor_tensor(prod[:, :, :, K0], g[:, :, D:D + H0], ew.to_broadcast([P, CH, H0]), ALU.mult)
                    nc.vector.tensor_copy(prod[:, :, :, K0 + 1], vbias[:, u, :].unsqueeze(2).to_broadcast([P, CH, H0])).then_inc(prods, 1)
                    nc.vector.tensor_scalar(att[:, 0, :], top[:], lk[:, u, 0:1], None, ALU.min)
                    v.wait_ge(prods, c + 3)
                    nc.vector.tensor_reduce(att[:, 1:CH + 1, :], prod[:], AX.X, ALU.add).then_inc(logits, 1)
                    v.wait_ge(logits, c + 1)
                    nc.vector.tensor_reduce(top[:], att[:].rearrange("p s h -> p h s"), AX.X, ALU.max).then_inc(maxed, 1)
                    v.wait_ge(maxed, c + 1)
                    nc.vector.tensor_tensor(dif[:, u, :, :], att[:, 0:CH + 1, :],
                                            top[:].unsqueeze(1).to_broadcast([P, CH + 1, H0]), ALU.subtract).then_inc(dif_ready, 1)
                    b = (u - 1) % R
                    v.wait_ge(exps_ready, c + 1)
                    vals = gat[:, b, :, D + H0:].rearrange("p s (h k) -> p s h k", h=H0)
                    nc.vector.tensor_tensor(wv[:].rearrange("p s (h k) -> p s h k", h=H0), vals,
                                            exps[:, b, :, :].unsqueeze(3).to_broadcast([P, CH + 1, H0, K0 + 1]),
                                            ALU.mult).then_inc(weighted, 1)
                    v.wait_ge(weighted, c + 4)
                    nc.vector.tensor_reduce(gat[:, u, 0, D + H0:], wv[:].rearrange("p s f -> p f s"), AX.X,
                                            ALU.add).then_inc(acc_ready, 1)

        @block.scalar
        def _(a):
            a.wait_ge(vec.sem, at["weights"])
            a.wait_ge(zeroed, 3)
            iters = a.value_load(s["cnt"][0:1, 0:1], min_val=1, max_val=NCMAX // U - 2)
            a.wait_ge(x_turned, 4)
            nc.scalar.activation(xT[:, 0, :], ps_x[0:MX, 0:P], ACT.Copy).then_inc(xT_ready, 1)
            with a.Fori(0, iters) as i:
                blks = block_numbers(nc, a.engine, t, i, U, -1)
                for u in range(U):
                    c = i * U + u
                    a.wait_ge(m1_done, c + 1)
                    nc.scalar.activation(h1[:, u % 2, :], ps_1[:, 0:HID], ACT.Relu, scale=0.99).then_inc(relu1_done, 1)
                    a.wait_ge(m2_done, c + 1)
                    b = (u - 1) % 2
                    nc.scalar.activation(h2[:, b, :], ps_2[:, b, 0:HID], ACT.Relu, scale=0.99).then_inc(relu2_done, 1)
                    a.wait_ge(x_turned, c + 5)
                    nc.scalar.activation(xT[:, (u + 1) % R, :], ps_x[0:MX, 0:P], ACT.Copy).then_inc(xT_ready, 1)
                    a.wait_ge(dif_ready, c + 1)
                    nc.scalar.activation(exps[:, u, :, :], dif[:, u, :, :], ACT.Exp).then_inc(exps_ready, 1)
                    a.wait_ge(acc_ready, c + 1)
                    a.wait_ge(acc_kept, c + 1)
                    nc.scalar.activation(flat(last[:, bass.ds(blks[u], 1), :]), gat[:, u, 0, D + H0:], ACT.Copy).then_inc(acc_kept, 1)

        @block.tensor
        def _(pe):
            pe.wait_ge(vec.sem, at["w1n"])
            nc.tensor.matmul(ps_3[0:MX, 0:P], flat(w1n[:]), w2T[:], start=True, stop=True)
            mat(nc.tensor.matmul(ps_3[0:MX, P:2 * P], vrow[:], b2r[:], start=True, stop=True))
            pe.wait_ge(vec.sem, at["weights"])
            iters = pe.value_load(s["cnt"][0:1, 0:1], min_val=1, max_val=NCMAX // U - 2)

            def turn(m):
                nc.tensor.transpose(ps_x[0:MX, 0:P], flat(xm[:, m, :, :]), s["ident"][:]).then_inc(x_turned, 1)

            pe.wait_ge(masks_ready, 1)
            turn(0)
            with pe.Fori(0, iters) as i:
                for u in range(U):
                    c = i * U + u
                    pe.wait_ge(relu1_done, c + 1)
                    pe.wait_ge(xT_ready, c + 1)
                    for k in range(CH):
                        mm = nc.tensor.matmul(ps_1[:, k * P:(k + 1) * P], w1x[:, k, :], xT[:, u, :], start=True, stop=True)
                    mm.then_inc(m1_done, 1)
                    b = (u - 1) % 2
                    for lo, hi in ((0, 4), (4, CH)):
                        nc.tensor.matmul(ps_2[:, b, lo * P:hi * P], w2T[:], h1[:, b, lo * P:hi * P], start=True, stop=False)
                        for k in range(lo, hi):
                            mm = nc.tensor.matmul(ps_2[:, b, k * P:(k + 1) * P], w2x[:, k, :], xT[:, (u - 1) % R, :],
                                                  start=False, stop=(k == hi - 1))
                    mm.then_inc(m2_done, 1)
                    pe.wait_ge(leaky_done, c + 1)
                    for k in range(CH):
                        mm = nc.tensor.matmul(ps_3[:, 0:P], w3T[:], h2[:, u % 2, k * P:(k + 1) * P],
                                              start=(k == 0), stop=(k == CH - 1))
                        if k == 0:
                            turn((u + 1) % R)
                    mm.then_inc(m3_done, 1)

        @block.gpsimd
        def _(p):
            nc.gpsimd.iota(io[:], [[1, CH]], base=0, channel_multiplier=0, allow_small_or_imprecise_dtypes=True).then_inc(iotas, 1)
            nc.gpsimd.iota(sio[:], [[-6, CH]], base=0, channel_multiplier=1, allow_small_or_imprecise_dtypes=True).then_inc(iotas, 1)
            nc.gpsimd.memset(gat[:], 0.0).then_inc(zeroed, 1)
            nc.gpsimd.memset(last[:], 0.0).then_inc(zeroed, 1)
            nc.gpsimd.memset(msg[:], 0.0).then_inc(zeroed, 1)

            def records(m):
                nc.gpsimd.indirect_dma_start(out=rec[:, m, :], out_offset=None, in_=t["recs"],
                                             in_offset=bass.IndirectOffsetOnAxis(ap=tab[:, m, 0:1], axis=0)).then_inc(rec_in[m], 16)

            iters = p.value_load(s["cnt"][0:1, 0:1], min_val=1, max_val=NCMAX // U - 2)
            p.wait_ge(vec.sem, at["cleared"])
            for m in range(3):
                p.wait_ge(tab_in[m], 16)
                records(m)
            with p.Fori(0, iters) as i:
                for u in range(U):
                    c = i * U + u
                    p.wait_ge(idx_ready, c + 1)
                    p.wait_ge(weighted, c + 1)
                    p.sem_inc(passed, 1)
                    for k in range(CH):
                        nc.gpsimd.indirect_dma_start(out=gat[:, u, 1 + k, :], out_offset=None, in_=t["row0"],
                                                     in_offset=bass.IndirectOffsetOnAxis(ap=meta[:, u, k:k + 1], axis=0)).then_inc(rows_in[u], 16)
                    m = (u + 3) % R
                    p.wait_ge(tab_in[m], i * 16 + (16 if u < R - 3 else 32))
                    p.wait_ge(prods, c + 2)
                    p.sem_inc(passed, 1)
                    records(m)
            for u in range(R):
                p.wait_ge(rec_in[u], iters * 16 + (16 if u < 3 else 0))
                p.wait_ge(tab_in[u], iters * 16 + 16)
                p.wait_ge(meta_out[u], iters * 16 + (32 if u <= 1 else 16))
            p.sem_inc(passed, 1)

        @block.sync
        def _(sp):
            n = 0
            sp.wait_ge(vec.sem, at["cleared"])
            for tile, a in ([(w1b[6 * k:6 * k + 5, :], w["L1_gnn_Wm1T"]) for k in range(CH)]
                            + [(w1b[6 * k + 5:6 * k + 6, :], w["L1_gnn_bm1"].rearrange("(a n) -> a n", a=1)) for k in range(CH)]
                            + [(w1n[:, 0, 0:5], w["L1_gnn_Wm1"]), (w1n[:, 0, 5:6], w["L1_gnn_bm1"].rearrange("(n a) -> n a", a=1)),
                               (w2T[:], w["L1_gnn_Wm2T"]), (w3T[:], w["L1_gnn_Wm3T"]),
                               (b2r[:], w["L1_gnn_bm2"].rearrange("(a n) -> a n", a=1))]):
                sp.dma_start(tile, a).then_inc(w_in, 16)
                n += 16
            assert n == at["w_in"]
            for m in range(R):
                sp.dma_start(t["meta"][NCMAX - 1], meta[:, m, :]).then_inc(meta_out[m], 16)
                sp.wait_ge(meta_out[m], 16)
                sp.dma_start(tab[:, m, :], t["tab"][:, 4 * m:4 * m + 4]).then_inc(tab_in[m], 16)
            iters = sp.value_load(s["cnt"][0:1, 0:1], min_val=1, max_val=NCMAX // U - 2)
            sp.wait_ge(masks_ready, 1)
            sp.dma_start(t["meta"][0], meta[:, 0, :]).then_inc(meta_out[0], 16)
            with sp.Fori(0, iters) as i:
                for u in range(U):
                    c = i * U + u
                    m = (u + 1) % R
                    ahead = sp.snap(c * 4 + 4 * U)
                    mine = sp.snap(c + 1)
                    sp.wait_ge(masks_ready, c + 2)
                    sp.dma_start(t["meta"][bass.ds(mine, 1)].rearrange("a p w -> p (a w)"), meta[:, m, :]).then_inc(meta_out[m], 16)
                    sp.dma_start(tab[:, u, :], t["tab"][:, bass.ds(ahead, 4)]).then_inc(tab_in[u], 16)
            behind = sp.snap(iters * U + 1)
            sp.wait_ge(summed, iters * U)
            sp.dma_start(t["meta"][bass.ds(behind, U - 1)].rearrange("a p w -> p a w"), meta[:, 1:U, :]).then_inc(meta_out[1], 16)


def node_mlp(nc, t, s, w):
    with ExitStack() as ctx:
        def sb(name, shape, dt=F32):
            return ctx.enter_context(nc.sbuf_tensor(f"{name}_n1", shape, dt))

        def sem(name):
            return nc.alloc_semaphore(f"{name}_n1")

        def psum(name, width):
            return ctx.enter_context(nc.psum_tensor(f"{name}_n1", [P, width], F32))

        G = 2
        STEPS = NB // G
        GP = G * P
        M1 = (P, U1 - P)
        M2 = (P, U2 - P)
        h, ag = s["tgt"], s["msg"]
        rden = sb("rden", [P, NB, H0])
        st6 = sb("st6", [P, 2, NB, 6])
        mv = sb("mv", [P, 2, NB, 2])
        rstd = sb("rstd", [P, NB])
        mean = sb("mean", [P, NB])
        half = sb("half_difference", [P, NB])
        stage = sb("msg_block", [P, 2, P])
        bm3 = sb("bm3", [P, D])
        bu3 = sb("bu3", [P, D])
        w1n = sb("wu1_natural", [P, 2, U1])
        w1 = sb("wu1", [P, 2, U1])
        w2 = sb("wu2", [P, 2, U2])
        w3 = sb("wu3", [P, 2, D])
        g = sb("ln_g", [P, 2])
        b = sb("ln_b", [P, 2])
        b1 = sb("b1", [P, 2])
        b2 = sb("b2", [P, 2])
        xn = sb("cat_norm", [P, G, 2, P])
        catT = sb("catT", [P, 2, GP])
        z1 = sb("z1", [P, 2, GP])
        z2 = sb("z2", [P, 2, GP])
        u1 = sb("u1", [P, 2, GP])
        u2 = sb("u2", [P, 2, GP])
        ps_t, ps_1, ps_2, ps_3, ps_m = psum("ps_t", 512), psum("ps_1", 512), psum("ps_2", 512), psum("ps_3", 512), psum("ps_m", 1024)

        ld = sem("w_in")
        vec, mat, sq = Tick(sem("vec")), Tick(sem("mat")), Tick(sem("sqrts"))
        row1, row2, row3 = sem("row1"), sem("row2"), sem("row3")
        bn1, bn2, normed, staged, turned, summed = (sem(n) for n in ("bn1", "bn2", "normed", "staged", "turned", "summed"))
        xn_ready, cat_turned, cat_ready = sem("xn_ready"), sem("cat_turned"), sem("cat_ready")
        z1_mm, z1_ready, u1_ready = sem("z1_mm"), sem("z1_ready"), sem("u1_ready")
        z2_mm, z2_ready, u2_ready = sem("z2_mm"), sem("z2_ready"), sem("u2_ready")
        out_mm, x_ready = sem("out_mm"), sem("x_ready")
        at = {}
        block = ctx.enter_context(nc.Block())

        def spread(a):
            return bass.AP(tensor=a.tensor, offset=0, ap=[[0, P], [1, D]])

        def column(a, o, n):
            return a.rearrange("(d a) -> d a", a=1)[o:o + n, :]

        loads = [(bm3[:], spread(w["L1_gnn_bm3"])), (bu3[:], spread(w["L1_gnn_bu3"]))]
        for k in range(2):
            lo = k * P
            loads += [(w1n[:, k, :], w["L1_gnn_Wu1T"][lo:lo + P, :]), (g[:, k:k + 1], column(w["L1_gnn_ln_g"], lo, P)),
                      (b[:, k:k + 1], column(w["L1_gnn_ln_b"], lo, P)),
                      (w2[0:M1[k], k, :], w["L1_gnn_Wu2T"][lo:lo + M1[k], :]),
                      (w3[0:M2[k], k, :], w["L1_gnn_Wu3T"][lo:lo + M2[k], :]),
                      (b1[0:M1[k], k:k + 1], column(w["L1_gnn_bu1"], lo, M1[k])),
                      (b2[0:M2[k], k:k + 1], column(w["L1_gnn_bu2"], lo, M2[k]))]

        def each_step(engine, step):
            for j in range(-1, 2):
                step(j)
            with engine.Fori(2, STEPS - 2) as j:
                step(j)
            for j in range(STEPS - 2, STEPS + 2):
                step(j)

        def has(j):
            return not isinstance(j, int) or 0 <= j < STEPS

        @block.sync
        def _(sp):
            for o, i in loads:
                sp.dma_start(o, i).then_inc(ld, 16)

        @block.vector
        def _(v):
            def do(ins, key=None):
                n = vec(ins)
                v.wait_ge(vec.sem, n)
                if key:
                    at[key] = n

            acc = s["acc"][:].rearrange("p b (h k) -> p b h k", h=H0)
            xs = s["xp"][:, 0:NB, :]
            do(nc.vector.tensor_scalar(rden[:], acc[:, :, :, K0], 1e-30, None, ALU.max))
            do(nc.vector.reciprocal(rden[:], rden[:]))
            do(nc.vector.tensor_tensor(acc[:, :, :, 0:K0], acc[:, :, :, 0:K0], rden[:].unsqueeze(3).to_broadcast([P, NB, H0, K0]), ALU.mult))
            xh = xs.rearrange("p b (h k) -> p b h k", h=H0)
            do(nc.vector.scalar_tensor_tensor(xh, acc[:, :, :, 0:K0], 0.0, xh, ALU.max, ALU.add))
            with v.Fori(0, NB // 10) as i:
                for u in range(10):
                    k = i * 10 + u
                    nc.vector.bn_stats(flat(st6[:, 0, bass.ds(k, 1), :]), flat(s["xp"][:, bass.ds(k, 1), :])).then_inc(bn1, 1)
            v.wait_ge(bn1, NB)
            row_stats(nc, v, st6[:, 0, :, :], mv[:, 0, :, :], row1, D)
            v.wait_ge(sq.sem, 1)
            do(nc.vector.reciprocal(rstd[:], rstd[:]))
            with v.Fori(0, NB // 10) as i:
                for u in range(10):
                    k = i * 10 + u
                    nc.vector.tensor_scalar(flat(h[:, bass.ds(k, 1), :]), flat(s["xp"][:, bass.ds(k, 1), :]),
                                            mv[:, 0, bass.ds(k, 1), 0:1].rearrange("p a b -> p (a b)"), rstd[:, bass.ds(k, 1)],
                                            ALU.subtract, ALU.mult).then_inc(normed, 1)
            v.wait_ge(normed, NB)
            do(nc.vector.tensor_scalar(h[:], h[:], 0.0, None, ALU.max))
            v.wait_ge(ld, 16 * len(loads))
            with v.Fori(0, NB // 10) as i:
                for u in range(10):
                    n, k = i * 10 + u, u % 2
                    v.wait_ge(turned, n + 3)
                    nc.vector.scalar_tensor_tensor(flat(ag[:, bass.ds(n, 1), :]), bm3[:], s["degp"][:, bass.ds(n, 1)],
                                                   ps_m[:, 512 * k:512 * k + P], ALU.mult, ALU.add).then_inc(summed, 1)
            v.wait_ge(summed, NB + 2)
            with v.Fori(0, NB // 10) as i:
                for u in range(10):
                    k = i * 10 + u
                    nc.vector.bn_stats(flat(st6[:, 0, bass.ds(k, 1), :]), flat(h[:, bass.ds(k, 1), :])).then_inc(bn2, 1)
                    nc.vector.bn_stats(flat(st6[:, 1, bass.ds(k, 1), :]), flat(ag[:, bass.ds(k, 1), :])).then_inc(bn2, 1)
            v.wait_ge(bn2, 2 * NB)
            row_stats(nc, v, st6[:, 0, :, :], mv[:, 0, :, :], row2, D)
            row_stats(nc, v, st6[:, 1, :, :], mv[:, 1, :, :], row3, D)
            do(nc.vector.tensor_tensor(mean[:], mv[:, 0, :, 0], mv[:, 1, :, 0], ALU.add))
            do(nc.vector.tensor_tensor(half[:], mv[:, 0, :, 0], mv[:, 1, :, 0], ALU.subtract))
            do(nc.vector.tensor_scalar(mean[:], mean[:], 0.5, None, ALU.mult))
            do(nc.vector.tensor_tensor(half[:], half[:], half[:], ALU.mult))
            do(nc.vector.tensor_tensor(mv[:, 0, :, 1], mv[:, 0, :, 1], mv[:, 1, :, 1], ALU.add))
            do(nc.vector.tensor_scalar(half[:], half[:], 0.25, None, ALU.mult))
            do(nc.vector.scalar_tensor_tensor(half[:], mv[:, 0, :, 1], 0.5, half[:], ALU.mult, ALU.add), "var")
            for k in range(2):
                do(nc.vector.tensor_scalar(w1[:, k, :], w1n[:, k, :], g[:, k:k + 1], None, ALU.mult), "w1")
            v.wait_ge(mat.sem, 1)
            for k in range(2):
                do(nc.vector.tensor_tensor(b1[0:M1[k], k:k + 1], b1[0:M1[k], k:k + 1], ps_t[0:M1[k], k:k + 1], ALU.add), "b1")
            v.wait_ge(sq.sem, 2)
            do(nc.vector.reciprocal(rstd[:], rstd[:]))

            def norm(j):
                for q in range(G):
                    n = j * G + q
                    for part, half_of in enumerate((h, ag)):
                        last = nc.vector.tensor_scalar(xn[:, q, part, :], flat(half_of[:, bass.ds(n, 1), :]),
                                                       mean[:, bass.ds(n, 1)], rstd[:, bass.ds(n, 1)], ALU.subtract, ALU.mult)
                last.then_inc(xn_ready, 1)

            norm(0)

            def step(j):
                if has(j - 2):
                    v.wait_ge(out_mm, j - 1)
                    for q in range(G):
                        n = (j - 2) * G + q
                        xb = flat(s["xp"][:, bass.ds(n, 1), :])
                        nc.vector.tensor_tensor(xb, xb, ps_3[:, q * P:(q + 1) * P], ALU.add).then_inc(x_ready, 1)
                if has(j - 1):
                    v.wait_ge(z2_ready, j)
                    for k in range(2):
                        ins = nc.vector.scalar_tensor_tensor(u2[0:M2[k], k, :], z2[0:M2[k], k, :], 0.01, z2[0:M2[k], k, :], ALU.mult, ALU.max)
                    ins.then_inc(u2_ready, 1)
                if has(j):
                    v.wait_ge(z1_ready, j + 1)
                    for k in range(2):
                        ins = nc.vector.scalar_tensor_tensor(u1[0:M1[k], k, :], z1[0:M1[k], k, :], 0.01, z1[0:M1[k], k, :], ALU.mult, ALU.max)
                    ins.then_inc(u1_ready, 1)
                if has(j + 2):
                    v.wait_ge(cat_turned, j + 2)
                    norm(j + 2)

            each_step(v, step)
            v.wait_ge(x_ready, G * STEPS)
            do(nc.vector.tensor_tensor(xs, xs, bu3[:].unsqueeze(1).to_broadcast([P, NB, D]), ALU.add))

        @block.scalar
        def _(a):
            a.wait_ge(row1, 6)
            sq(nc.scalar.activation(rstd[:], mv[:, 0, :, 1], ACT.Sqrt, bias=s["eps"][:, 0:1]))
            a.sem_inc(turned, 2)
            with a.Fori(0, NB // 10) as i:
                for u in range(10):
                    n, k = i * 10 + u, u % 2
                    a.wait_ge(turned, n + 1)
                    nc.scalar.activation(stage[:, k, :], flat(ag[:, bass.ds(n, 1), :]), ACT.Copy).then_inc(staged, 1)
            a.wait_ge(vec.sem, at["var"])
            sq(nc.scalar.activation(rstd[:], half[:], ACT.Sqrt, bias=s["eps"][:, 0:1]))
            a.wait_ge(vec.sem, at["b1"])

            def step(j):
                if has(j - 1):
                    a.wait_ge(z2_mm, j)
                    for k in range(2):
                        ins = nc.scalar.activation(z2[0:M2[k], k, :], ps_2[0:M2[k], k * GP:(k + 1) * GP], ACT.Identity, bias=b2[0:M2[k], k:k + 1])
                    ins.then_inc(z2_ready, 1)
                if has(j):
                    a.wait_ge(z1_mm, j + 1)
                    for k in range(2):
                        ins = nc.scalar.activation(z1[0:M1[k], k, :], ps_1[0:M1[k], k * GP:(k + 1) * GP], ACT.Identity, bias=b1[0:M1[k], k:k + 1])
                    ins.then_inc(z1_ready, 1)
                if has(j + 1):
                    a.wait_ge(cat_turned, j + 2)
                    nc.scalar.activation(flat(catT[:]), ps_t[:, 0:2 * GP], ACT.Copy).then_inc(cat_ready, 1)

            each_step(a, step)

        @block.tensor
        def _(pe):
            pe.sem_inc(summed, 2)
            with pe.Fori(0, NB // 10) as i:
                for u in range(10):
                    n, k = i * 10 + u, u % 2
                    pe.wait_ge(staged, n + 1)
                    pe.wait_ge(summed, n + 1)
                    nc.tensor.transpose(ps_m[:, 512 * k:512 * k + P], stage[:, k, :], s["ident"][:]).then_inc(turned, 1)
            pe.wait_ge(ld, 16 * len(loads))
            for m in range(2):
                for k in range(2):
                    mm = nc.tensor.matmul(ps_t[0:M1[m], m:m + 1], w1n[:, k, m * P:m * P + M1[m]], b[:, k:k + 1], start=(k == 0), stop=(k == 1))
            mat(mm)
            pe.wait_ge(vec.sem, at["b1"])

            def step(j):
                if has(j - 2):
                    pe.wait_ge(u2_ready, j - 1)
                    for q in range(G):
                        for k in range(2):
                            mm = nc.tensor.matmul(ps_3[:, q * P:(q + 1) * P], u2[0:M2[k], k, q * P:(q + 1) * P], w3[0:M2[k], k, :],
                                                  start=(k == 0), stop=(k == 1))
                    mm.then_inc(out_mm, 1)
                if has(j - 1):
                    pe.wait_ge(u1_ready, j)
                    for m in range(2):
                        for k in range(2):
                            mm = nc.tensor.matmul(ps_2[0:M2[m], m * GP:(m + 1) * GP], w2[0:M1[k], k, m * P:m * P + M2[m]], u1[0:M1[k], k, :],
                                                  start=(k == 0), stop=(k == 1))
                    mm.then_inc(z2_mm, 1)
                if has(j):
                    pe.wait_ge(cat_ready, j + 1)
                    for m in range(2):
                        for k in range(2):
                            mm = nc.tensor.matmul(ps_1[0:M1[m], m * GP:(m + 1) * GP], w1[:, k, m * P:m * P + M1[m]], catT[:, k, :],
                                                  start=(k == 0), stop=(k == 1))
                    mm.then_inc(z1_mm, 1)
                if has(j + 1):
                    pe.wait_ge(xn_ready, j + 2)
                    for q in range(G):
                        for k in range(2):
                            o = k * GP + q * P
                            mm = nc.tensor.transpose(ps_t[:, o:o + P], xn[:, q, k, :], s["ident"][:])
                    mm.then_inc(cat_turned, 1)

            each_step(pe, step)


def edge_attention(nc, t, s, layer, w, out):
    with ExitStack() as ctx:
        def sb(name, shape, dt=F32):
            return ctx.enter_context(nc.sbuf_tensor(f"{name}_e{layer}", shape, dt))

        def sem(name):
            return nc.alloc_semaphore(f"{name}_e{layer}")

        R = U
        tab = sb("tab", [P, R, 4], I32)
        meta = sb("meta", [P, R, 2 * CH], I32)
        vbias = sb("vbias", [P, CH])
        gat = sb("gathered", [P, R, CH + 1, ROW2])
        z = sb("z", [P, CH, H2, K2])
        az = sb("abs_z", [P, CH, H2, K2])
        prod = sb("prod", [P, CH, H2, K2 + 3])
        att = sb("att", [P, CH + 2, H2])
        dif = sb("dif", [P, CH + 1, H2])
        exps = sb("exps", [P, CH + 1, H2])
        wv = sb("wv", [P, CH + 1, V2])
        io = sb("slot_no", [P, CH])
        attw = sb("attw", [P, D])
        web = sb("web", [P, H2])
        bias = sb("bias", [P, D])
        rden = sb("rden", [P, NB, H2])
        loop_logit = sb("loop_logit", [P, NB, H2])
        merged = sb("merged", [P, NB, H2])
        e_sum = sb("exp_sum", [P, NB, H2])
        e_loop = sb("exp_loop", [P, NB, H2])
        big = s["msg"]
        acc = s["acc"][:, :, 0:V2]

        tab_in = [sem(f"tab_in{u}") for u in range(R)]
        meta_in = [sem(f"meta_in{u}") for u in range(R)]
        rows_in = [sem(f"rows_in{u}") for u in range(R)]
        w_in, iotas, passed = sem("w_in"), sem("iotas"), sem("passed")
        vec = Tick(sem("vec"))
        z_ready, abs_ready, prods, logits, maxed, dif_ready = (sem(n) for n in ("z_ready", "abs_ready", "prods", "logits", "maxed", "dif_ready"))
        exps_ready, weighted, acc_ready, acc_kept = (sem(n) for n in ("exps_ready", "weighted", "acc_ready", "acc_kept"))
        slots_summed = sem("slots_summed")
        ps = ctx.enter_context(nc.psum_tensor(f"ps_e{layer}", [P, 512], F32))
        scattered, loop_abs, loop_exps = sem("scattered"), sem("loop_abs"), sem("loop_exps")
        at = {}
        block = ctx.enter_context(nc.Block())

        def spread(a, n):
            return bass.AP(tensor=a.tensor, offset=0, ap=[[0, P], [1, n]])

        loads = [(bias[:], spread(w[f"L{layer}_gnn_bias"], D))]
        if layer == 2:
            loads += [(attw[:], spread(w["L2_gnn_att"], D)), (web[:], spread(w["L2_gnn_W_eb"], H2))]

        @block.vector
        def _(v):
            def do(ins, key=None):
                n = vec(ins)
                v.wait_ge(vec.sem, n)
                if key:
                    at[key] = n

            for tile in (gat, att, exps):
                do(nc.vector.memset(tile[:], 0.0))
            do(nc.vector.memset(att[:, CH + 1, :], FLOOR))
            v.wait_ge(w_in, 16 * len(loads))
            v.wait_ge(iotas, 1)
            if layer == 2:
                do(nc.vector.tensor_scalar(attw[:], attw[:], 0.4, None, ALU.mult))
                v.wait_ge(loop_abs, 1)
                bh = big[:].rearrange("p b (h k) -> p b h k", h=H2)
                do(nc.vector.tensor_tensor(big[:], big[:], attw[:].unsqueeze(1).to_broadcast([P, NB, D]), ALU.mult))
                do(nc.vector.tensor_reduce(loop_logit[:], bh, AX.X, ALU.add))
                do(nc.vector.tensor_tensor(loop_logit[:], loop_logit[:], s["tsc"][:], ALU.add))
                do(nc.vector.scalar_tensor_tensor(loop_logit[:], loop_logit[:], 2.0, web[:].unsqueeze(1).to_broadcast([P, NB, H2]),
                                                  ALU.mult, ALU.add))
            v.sem_inc(weighted, 3)
            v.sem_inc(exps_ready, 1)
            v.sem_inc(acc_kept, 1)
            v.sem_inc(acc_ready, 1)
            at["start"] = vec.n
            iters = v.value_load(s["cnt"][0:1, 0:1], min_val=1, max_val=NCMAX // U - 2)
            with v.Fori(0, iters) as i:
                blks = block_numbers(nc, v.engine, t, i, U, 0)
                for u in range(U):
                    c = i * U + u
                    g = gat[:, u, 1:CH + 1, :]
                    left = tab[:].bitcast(F32)[:, u, 1:2]
                    score = s["tsc"][:, bass.ds(blks[u], 1), :].to_broadcast([P, CH, H2])
                    v.wait_ge(tab_in[u], i * 16 + 16)
                    v.wait_ge(meta_in[u], i * 16 + 16)
                    v.wait_ge(rows_in[u], i * (16 * CH) + 16 * CH)
                    if layer == 2:
                        q = flat(s["tgt"][:, bass.ds(blks[u], 1), :]).rearrange("p (h k) -> p h k", h=H2)
                        nc.vector.tensor_tensor(z[:], g[:, :, 0:V2].rearrange("p s (h k) -> p s h k", h=H2)[:, :, :, 0:K2],
                                                q.unsqueeze(1).to_broadcast([P, CH, H2, K2]), ALU.add).then_inc(z_ready, 1)
                        nc.vector.tensor_scalar(vbias[:], io[:], left, -BIG, ALU.is_ge, ALU.mult).then_inc(logits, 1)
                    else:
                        nc.vector.tensor_tensor(z[:, :, :, 0], g[:, :, V2:], score, ALU.add).then_inc(z_ready, 1)
                        nc.vector.tensor_scalar(vbias[:], io[:], left, -BIG, ALU.is_ge, ALU.mult).then_inc(logits, 1)
                    b = (u - 1) % R
                    v.wait_ge(exps_ready, c + 1)
                    v.wait_ge(acc_ready, c + 1)
                    vals = gat[:, b, :, 0:V2].rearrange("p s (h k) -> p s h k", h=H2)
                    nc.vector.tensor_tensor(wv[:].rearrange("p s (h k) -> p s h k", h=H2), vals,
                                            exps[:].unsqueeze(3).to_broadcast([P, CH + 1, H2, K2 + 1]), ALU.mult).then_inc(weighted, 1)
                    nc.vector.tensor_scalar(att[:, 0, :], gat[:, u, 0, V2:], tab[:].bitcast(F32)[:, u, 2:3], None, ALU.min)
                    v.wait_ge(logits, c * 2 + 1)
                    if layer == 2:
                        nc.vector.tensor_tensor(prod[:, :, :, K2], g[:, :, V2:], score, ALU.add)
                        red = meta[:].bitcast(F32)[:, u, CH:2 * CH]
                        nc.vector.tensor_tensor(prod[:, :, :, K2 + 1], web[:].unsqueeze(1).to_broadcast([P, CH, H2]),
                                                red.unsqueeze(2).to_broadcast([P, CH, H2]), ALU.mult)
                        nc.vector.tensor_copy(prod[:, :, :, K2 + 2], vbias[:].unsqueeze(2).to_broadcast([P, CH, H2]))
                        v.wait_ge(abs_ready, c + 1)
                        aw = attw[:].rearrange("p (h k) -> p h k", h=H2).unsqueeze(1).to_broadcast([P, CH, H2, K2])
                        nc.vector.tensor_tensor(prod[:, :, :, 0:K2], az[:], aw, ALU.mult).then_inc(prods, 1)
                        v.wait_ge(prods, c + 1)
                        nc.vector.tensor_reduce(att[:, 1:CH + 1, :], prod[:], AX.X, ALU.add).then_inc(logits, 1)
                    else:
                        v.wait_ge(z_ready, c + 1)
                        nc.vector.scalar_tensor_tensor(az[:, :, :, 0], z[:, :, :, 0], 0.2, z[:, :, :, 0], ALU.mult, ALU.max).then_inc(prods, 1)
                        v.wait_ge(prods, c + 1)
                        nc.vector.tensor_tensor(att[:, 1:CH + 1, :], az[:, :, :, 0], vbias[:].unsqueeze(2).to_broadcast([P, CH, H2]),
                                                ALU.add).then_inc(logits, 1)
                    v.wait_ge(logits, c * 2 + 2)
                    top = gat[:, (u + 1) % R, 0, V2:]
                    nc.vector.tensor_reduce(top, att[:].rearrange("p s h -> p h s"), AX.X, ALU.max).then_inc(maxed, 1)
                    v.wait_ge(maxed, c + 1)
                    nc.vector.tensor_tensor(dif[:], att[:, 0:CH + 1, :], top.unsqueeze(1).to_broadcast([P, CH + 1, H2]),
                                            ALU.subtract).then_inc(dif_ready, 1)
            v.wait_ge(acc_kept, iters * U + 1)
            xs = s["xp"][:, 0:NB, :]
            ah = acc.rearrange("p b (h k) -> p b h k", h=H2)
            if layer == 2:
                top = s["acc"][:, :, V2:ROW2]
                do(nc.vector.tensor_tensor(merged[:], top, loop_logit[:], ALU.max))
                do(nc.vector.tensor_tensor(e_sum[:], top, merged[:], ALU.subtract))
                do(nc.vector.tensor_tensor(e_loop[:], loop_logit[:], merged[:], ALU.subtract), "merged")
                v.wait_ge(loop_exps, 2)
                do(nc.vector.tensor_tensor(ah, ah, e_sum[:].unsqueeze(3).to_broadcast([P, NB, H2, K2 + 1]), ALU.mult))
                do(nc.vector.tensor_tensor(bh, s["tgt"][:].rearrange("p b (h k) -> p b h k", h=H2),
                                           e_loop[:].unsqueeze(3).to_broadcast([P, NB, H2, K2]), ALU.mult))
                do(nc.vector.tensor_tensor(ah[:, :, :, K2], ah[:, :, :, K2], e_loop[:], ALU.add))
                do(nc.vector.tensor_tensor(ah[:, :, :, 0:K2], ah[:, :, :, 0:K2], bh, ALU.add))
                do(nc.vector.tensor_scalar(rden[:], ah[:, :, :, K2], 1e-12, None, ALU.max))
            else:
                do(nc.vector.tensor_scalar(rden[:], ah[:, :, :, K2], 1e-16, None, ALU.add))
            do(nc.vector.reciprocal(rden[:], rden[:]))
            do(nc.vector.tensor_tensor(ah[:, :, :, 0:K2], ah[:, :, :, 0:K2], rden[:].unsqueeze(3).to_broadcast([P, NB, H2, K2]), ALU.mult))
            do(nc.vector.tensor_tensor(xs, xs, bias[:].unsqueeze(1).to_broadcast([P, NB, D]), ALU.add))
            xh = xs.rearrange("p b (h k) -> p b h k", h=H2)
            do(nc.vector.tensor_tensor(xh, xh, ah[:, :, :, 0:K2], ALU.add), "x")

        @block.scalar
        def _(a):
            if layer == 2:
                nc.scalar.activation(big[:], s["tgt"][:], ACT.Abs).then_inc(loop_abs, 1)
            a.wait_ge(vec.sem, at["start"])
            iters = a.value_load(s["cnt"][0:1, 0:1], min_val=1, max_val=NCMAX // U - 2)
            with a.Fori(0, iters) as i:
                blks = block_numbers(nc, a.engine, t, i, U, -1)
                for u in range(U):
                    c = i * U + u
                    if layer == 2:
                        a.wait_ge(z_ready, c + 1)
                        nc.scalar.activation(az[:], z[:], ACT.Abs).then_inc(abs_ready, 1)
                    a.wait_ge(slots_summed, c + 1)
                    nc.scalar.activation(gat[:, u, 0, 0:V2], ps[:, 0:V2], ACT.Copy).then_inc(acc_ready, 1)
                    a.wait_ge(acc_ready, c + 2)
                    a.wait_ge(acc_kept, c + 1)
                    nc.scalar.activation(flat(s["acc"][:, bass.ds(blks[u], 1), :]), gat[:, u, 0, :], ACT.Copy).then_inc(acc_kept, 1)
                    a.wait_ge(dif_ready, c + 1)
                    nc.scalar.activation(exps[:], dif[:], ACT.Exp).then_inc(exps_ready, 1)
            if layer == 2:
                a.wait_ge(vec.sem, at["merged"])
                nc.scalar.activation(e_sum[:], e_sum[:], ACT.Exp).then_inc(loop_exps, 1)
                nc.scalar.activation(e_loop[:], e_loop[:], ACT.Exp).then_inc(loop_exps, 1)

        @block.tensor
        def _(pe):
            pe.wait_ge(vec.sem, at["start"])
            iters = pe.value_load(s["cnt"][0:1, 0:1], min_val=1, max_val=NCMAX // U - 2)
            with pe.Fori(0, iters) as i:
                for u in range(U):
                    pe.wait_ge(weighted, i * U + u + 4)
                    for k in range(CH + 1):
                        mm = nc.tensor.matmul(ps[:, 0:V2], s["ident"][:], wv[:, k, :], start=(k == 0), stop=(k == CH))
                    mm.then_inc(slots_summed, 1)

        @block.gpsimd
        def _(p):
            nc.gpsimd.iota(io[:], [[1, CH]], base=0, channel_multiplier=0, allow_small_or_imprecise_dtypes=True).then_inc(iotas, 1)
            iters = p.value_load(s["cnt"][0:1, 0:1], min_val=1, max_val=NCMAX // U - 2)
            p.wait_ge(vec.sem, at["start"])
            with p.Fori(0, iters) as i:
                for u in range(U):
                    c = i * U + u
                    p.wait_ge(meta_in[u], i * 16 + 16)
                    p.wait_ge(weighted, c + 1)
                    p.sem_inc(passed, 1)
                    for k in range(CH):
                        nc.gpsimd.indirect_dma_start(out=gat[:, u, 1 + k, :], out_offset=None, in_=t[f"row{layer}"],
                                                     in_offset=bass.IndirectOffsetOnAxis(ap=meta[:, u, k:k + 1], axis=0)).then_inc(rows_in[u], 16)
            for u in range(R):
                p.wait_ge(tab_in[u], iters * 16 + 16)
                p.wait_ge(meta_in[u], iters * 16 + 16)
            p.sem_inc(passed, 1)
            if layer == 3:
                p.wait_ge(vec.sem, at["x"])
                for b in range(-(-N // P)):
                    n = min(P, N - b * P)
                    nc.gpsimd.indirect_dma_start(out=out, out_offset=bass.IndirectOffsetOnAxis(ap=s["nid"][0:n, b:b + 1], axis=0),
                                                 in_=s["xp"][0:n, b, :], in_offset=None).then_inc(scattered, 16)
                p.wait_ge(scattered, 16 * (-(-N // P)))

        @block.sync
        def _(sp):
            for o, i in loads:
                sp.dma_start(o, i).then_inc(w_in, 16)
            for u in range(R):
                sp.dma_start(tab[:, u, :], t["tab"][:, 4 * u:4 * u + 4]).then_inc(tab_in[u], 16)
                sp.dma_start(meta[:, u, :], t["meta"][u]).then_inc(meta_in[u], 16)
            iters = sp.value_load(s["cnt"][0:1, 0:1], min_val=1, max_val=NCMAX // U - 2)
            with sp.Fori(0, iters) as i:
                for u in range(U):
                    c = i * U + u
                    ahead = sp.snap(c * 4 + 4 * U)
                    mahead = sp.snap(c + U)
                    sp.wait_ge(logits, c * 2 + 2)
                    sp.dma_start(tab[:, u, :], t["tab"][:, bass.ds(ahead, 4)]).then_inc(tab_in[u], 16)
                    sp.dma_start(meta[:, u, :], t["meta"][bass.ds(mahead, 1)].rearrange("a p w -> p (a w)")).then_inc(meta_in[u], 16)


EDGES = ("x", "src", "dst", "edge_attr_2", "edge_attr_5", "edge_weight")
WEIGHTS = ("L0_gnn_Wk", "L0_gnn_bk", "L0_gnn_Wq", "L0_gnn_bq", "L0_gnn_Wv", "L0_gnn_bv", "L0_gnn_rel_att", "L0_gnn_rel_msg",
           "L1_gnn_Wm1", "L1_gnn_bm1", "L1_gnn_Wm2", "L1_gnn_bm2", "L1_gnn_Wm3", "L1_gnn_bm3", "L1_gnn_ln_g", "L1_gnn_ln_b",
           "L1_gnn_Wu1", "L1_gnn_bu1", "L1_gnn_Wu2", "L1_gnn_bu2", "L1_gnn_Wu3", "L1_gnn_bu3",
           "L2_gnn_W_lin", "L2_gnn_att", "L2_gnn_W_eb", "L2_gnn_bias", "L2_gnn_W_res",
           "L3_gnn_weight", "L3_gnn_att_weight", "L3_gnn_bias")
TURNED = ("L0_gnn_Wk", "L0_gnn_Wq", "L1_gnn_Wm1", "L1_gnn_Wm2", "L1_gnn_Wm3", "L1_gnn_Wu1", "L1_gnn_Wu2", "L1_gnn_Wu3",
          "L2_gnn_W_lin", "L2_gnn_W_res")


def kernel(**inputs):
    import numpy as _np
    import concourse.bacc as _bacc
    from concourse import mybir as _mybir
    from concourse.bass_utils import run_bass_kernel_spmd as _run

    arrays = {name: _np.ascontiguousarray(inputs[name]) for name in EDGES + WEIGHTS}
    for name in TURNED:
        arrays[name + "T"] = _np.ascontiguousarray(arrays[name].T)
    arrays["L3_gnn_weightT"] = _np.ascontiguousarray(arrays["L3_gnn_weight"].reshape(D, D).T)
    nc = _bacc.Bacc("TRN2", target_bir_lowering=False, num_devices=1)
    aps = {name: nc.dram_tensor(f"in_{name}", a.shape, _mybir.dt.from_np(a.dtype), kind="ExternalInput").ap()
           for name, a in arrays.items()}
    out = nc.dram_tensor("out_x", [N, D], F32, kind="ExternalOutput").ap()
    program(nc, None, *[aps[name] for name in EDGES[:3]], *[aps[name] for name in EDGES[3:]],
            {name: ap for name, ap in aps.items() if name.startswith("L")}, out)
    r = _run(nc, [{f"in_{name}": a for name, a in arrays.items()}], core_ids=[0])
    return r.results[0]["out_x"]
```
